# Optimizing a Trainium2 kernel written in Bass

```python
import numpy as np
import jax
import jax.numpy as jnp

def _softmax(x, axis=-1):
    return jax.nn.softmax(x, axis=axis)

def _gelu(x):
    return jax.nn.gelu(x, approximate=True)

def _silu(x):
    return jax.nn.silu(x)

def _sigmoid(x):
    return jax.nn.sigmoid(x)

def _layernorm(x, axis=-1, eps=1e-05):
    m = jnp.mean(x, axis=axis, keepdims=True)
    v = jnp.var(x, axis=axis, keepdims=True)
    return (x - m) / jnp.sqrt(v + eps)

def _scatter_add(tgt, idx, src, axis=0):
    return tgt.at[idx].add(src)

def _segment_sum(src, seg, n):
    return jax.ops.segment_sum(src, seg, n)
kernel_name = 'mk_gnn_ffn_d1_gnn_r8_933d51'

def setup_inputs(seed: int=0):
    np.random.seed(seed)
    _w = jnp.asarray

    def _rec_inputs():
        import jax
        import jax.numpy as jnp
        _gk = jax.random.key(seed)
        x = -8.776e-05 + 1 * jax.random.normal(jax.random.fold_in(_gk, 1), (1250, 512), jnp.float32)
        src = jax.random.randint(jax.random.fold_in(_gk, 2), (20000,), 0, 1250, jnp.int32)
        dst = jax.random.randint(jax.random.fold_in(_gk, 3), (20000,), 0, 1250, jnp.int32)
        _o = jnp.argsort(dst, stable=True)
        src = src[_o]
        dst = dst[_o]
        return (x, src, dst)
    x, src, dst = _rec_inputs()

    def _L0_gnn_setup():
        import jax, jax.numpy as jnp
        import numpy as np
        N_NODES = 1250
        N_EDGES = 20000
        D_IN = 512
        D_OUT = 512
        LEAKY_SLOPE = 0.01
        EPS = 1e-12
        key = jax.random.key(seed)
        k1, k2, k3, k4, k5, k6 = jax.random.split(key, 6)
        x = jax.random.normal(k1, (N_NODES, D_IN), dtype=jnp.float32)
        src = jax.random.randint(k2, (N_EDGES,), 0, N_NODES, dtype=jnp.int64)
        dst = jax.random.randint(k3, (N_EDGES,), 0, N_NODES, dtype=jnp.int64)
        scale = 1.0 / np.sqrt(D_IN)
        W_self = jax.random.normal(k4, (D_IN, D_OUT), dtype=jnp.float32) * scale
        W_neigh = jax.random.normal(k5, (D_IN, D_OUT), dtype=jnp.float32) * scale
        b = jax.random.normal(k6, (D_OUT,), dtype=jnp.float32) * scale
        return {'x': x, 'src': src, 'dst': dst, 'W_self': W_self, 'W_neigh': W_neigh, 'b': b}
    _L0_gnn_all = _L0_gnn_setup()
    _L0_gnn_in = {k: v for k, v in _L0_gnn_all.items() if k in ('W_self', 'W_neigh', 'b')}
    del _L0_gnn_all

    def _L0_ffn_setup():
        import jax, jax.numpy as jnp
        import numpy as np
        DIM = 512
        FFN_DIM = 1408
        GROUP = 128
        EPS = 1e-05

        def _quantize_weight(w, group_size):
            o, i = w.shape
            wg = w.reshape(o, i // group_size, group_size)
            scale = jnp.mean(jnp.abs(wg), axis=-1, keepdims=True) + EPS
            wq = jnp.clip(jnp.round(wg / scale), -1.0, 1.0) * scale
            return wq.reshape(o, i)

        def _bitlinear(x, w, group_size=GROUP):
            wq = w + jax.lax.stop_gradient(_quantize_weight(w, group_size) - w)
            return jnp.einsum('bsd,fd->bsf', x, wq)
        key = jax.random.key(seed)
        k_x, k_g, k_u, k_d = jax.random.split(key, 4)
        x = jax.random.normal(k_x, (8, 512, DIM), dtype=jnp.float32)
        sd_in = 1.0 / np.sqrt(DIM)
        sd_ffn = 1.0 / np.sqrt(FFN_DIM)
        w_gate = jax.random.normal(k_g, (FFN_DIM, DIM), dtype=jnp.float32) * sd_in
        w_up = jax.random.normal(k_u, (FFN_DIM, DIM), dtype=jnp.float32) * sd_in
        w_down = jax.random.normal(k_d, (DIM, FFN_DIM), dtype=jnp.float32) * sd_ffn
        return {'x': x, 'w_gate': w_gate, 'w_up': w_up, 'w_down': w_down}
    _L0_ffn_all = _L0_ffn_setup()
    _L0_ffn_in = {k: v for k, v in _L0_ffn_all.items() if k in ('w_gate', 'w_up', 'w_down')}
    del _L0_ffn_all
    return {'x': x, 'src': src, 'dst': dst, 'L0_gnn_W_self': _L0_gnn_in['W_self'], 'L0_gnn_W_neigh': _L0_gnn_in['W_neigh'], 'L0_gnn_b': _L0_gnn_in['b'], 'L0_ffn_w_gate': _L0_ffn_in['w_gate'], 'L0_ffn_w_up': _L0_ffn_in['w_up'], 'L0_ffn_w_down': _L0_ffn_in['w_down']}

def reference(x, src, dst, L0_gnn_W_self, L0_gnn_W_neigh, L0_gnn_b, L0_ffn_w_gate, L0_ffn_w_up, L0_ffn_w_down):
    import jax
    import jax.numpy as jnp

    def _L0_gnn_ref(x, src, dst, W_self, W_neigh, b):
        import jax, jax.numpy as jnp
        import numpy as np
        N_NODES = 1250
        N_EDGES = 20000
        D_IN = 512
        D_OUT = 512
        LEAKY_SLOPE = 0.01
        EPS = 1e-12
        msg_sum = jax.ops.segment_sum(x[src], dst, num_segments=N_NODES)
        deg = jax.ops.segment_sum(jnp.ones((src.shape[0],), x.dtype), dst, num_segments=N_NODES)
        neigh = msg_sum / jnp.maximum(deg, 1.0)[:, None]
        h = x @ W_self + neigh @ W_neigh + b
        h = jnp.where(h >= 0, h, LEAKY_SLOPE * h)
        norm = jnp.sqrt(jnp.sum(h * h, axis=1, keepdims=True))
        return h / jnp.maximum(norm, EPS)

    def _L0_ffn_ref(x, w_gate, w_up, w_down):
        import jax, jax.numpy as jnp
        import numpy as np
        DIM = 512
        FFN_DIM = 1408
        GROUP = 128
        EPS = 1e-05

        def _quantize_weight(w, group_size):
            o, i = w.shape
            wg = w.reshape(o, i // group_size, group_size)
            scale = jnp.mean(jnp.abs(wg), axis=-1, keepdims=True) + EPS
            wq = jnp.clip(jnp.round(wg / scale), -1.0, 1.0) * scale
            return wq.reshape(o, i)

        def _bitlinear(x, w, group_size=GROUP):
            wq = w + jax.lax.stop_gradient(_quantize_weight(w, group_size) - w)
            return jnp.einsum('bsd,fd->bsf', x, wq)
        gate = _bitlinear(x, w_gate)
        up = _bitlinear(x, w_up)
        h = jax.nn.silu(gate) * up
        return _bitlinear(h, w_down)
    x = x + _L0_gnn_ref(_layernorm(x, axis=-1), src, dst, L0_gnn_W_self, L0_gnn_W_neigh, L0_gnn_b)
    x = x + _L0_ffn_ref(_layernorm(x, axis=-1)[None], L0_ffn_w_gate, L0_ffn_w_up, L0_ffn_w_down)[0]
    return x

_drawn_inputs = setup_inputs


def setup_inputs(seed=0):
    import zlib

    import numpy as np

    out = dict(_drawn_inputs(seed))
    spreads = {}
    factors = {'L0_gnn_W_neigh': 5.211, 'L0_gnn_b': 8.0}
    for name, (base, spread) in spreads.items():
        noise = np.random.default_rng([zlib.crc32(name.encode()), seed]).standard_normal(out[name].shape)
        drawn = base * np.exp(spread * noise) if base else spread * noise
        out[name] = jnp.asarray(drawn.astype(out[name].dtype))
    for name, factor in factors.items():
        out[name] = (out[name] * factor).astype(out[name].dtype)
    return out
```

```python
from contextlib import ExitStack

import concourse.bass as bass
from concourse import mybir

F32 = mybir.dt.float32
F32R = mybir.dt.float32r
BF16 = mybir.dt.bfloat16
U16 = mybir.dt.uint16
I32 = mybir.dt.int32
ALU = mybir.AluOpType
ACT = mybir.ActivationFunctionType

P = 128
WIN = 48
ROUND = 12582912.0
LN_EPS = 1e-5
NORM_EPS = 1e-12
Q_EPS = 1e-5
SLOPE = 0.01


def gnn_ffn(nc, x, src, dst, w_self, w_neigh, bias, w_gate, w_up, w_down, out):
    N, D = x.shape
    E = src.shape[0]
    F = w_gate.shape[0]
    TP = 125
    NT = N // TP
    KD = D // P
    NF = F // P
    NC = -(-E // P)
    NCP = 160
    EPD = E // N
    STEP = P // EPD
    LEAD = (WIN - STEP) // 2
    NB = -(-N // WIN)
    assert (N, D, E, F) == (TP * NT, 512, EPD * N, 1408) and NC == 157 and WIN % STEP == 0

    HOT = 4
    RW = 4 * P
    RAWS = 4
    CH = [(0, 418), (418, 416), (834, 416)]
    CW = 424

    base = 17408
    at = {}
    for name, size in (
        ("x", NT * D * 4), ("tq_gu", 2 * NF * D * 2), ("tq_d", KD * F * 2), ("xz", NT * D * 4), ("raw", RAWS * RW * 4),
        ("w", KD * 2 * D * 4), ("hot", HOT * (NT * WIN + P) * 2), ("y", 2 * NT * D * 4), ("a", NT * N * 4),
        ("xn", 2 * D * 4), ("small", 12288),
    ):
        at[name] = base
        base += -(-size // 32) * 32
    assert base <= 229368, base
    used = {"small": 0}

    def place(name, shape, dt, region, offset=0):
        return nc.alloc_sbuf_tensor_at(name, shape, dt, offset=at[region] + offset)

    def small(name, shape, dt):
        width = {F32: 4, F32R: 4, I32: 4, BF16: 2, U16: 2}[dt]
        for n in shape[1:]:
            width *= n
        o = used["small"]
        used["small"] = o + -(-width // 32) * 32
        assert used["small"] <= 12288
        return place(name, shape, dt, "small", o)

    x_sb = place("x_sb", [TP, NT, D], F32, "x")
    tq_gu = place("tq_gu", [P, 2 * NF, D], BF16, "tq_gu")
    tq_d = place("tq_d", [P, KD, F], BF16, "tq_d")
    xnT = place("xnT", [P, NT, D], F32, "xz")
    z = place("z", [TP, NT, D], F32, "xz")
    raw = place("raw", [P, RAWS, RW], F32, "raw")
    w_sb = place("w_sb", [P, KD, 2 * D], F32, "w")
    hot_dst = place("hot_dst", [P, HOT, NT * WIN], BF16, "hot")
    hot_src = place("hot_src", [P, HOT, P], BF16, "hot", HOT * NT * WIN * 2)
    y_hi = place("y_hi", [TP, NT, D], F32R, "y")
    y_lo = place("y_lo", [TP, NT, D], F32R, "y", NT * D * 4)
    a_t = place("a_t", [TP, NT, N], F32R, "a")
    e_i = place("e_i", [P, 4, P], I32, "a")
    e_f = place("e_f", [P, 4, P], F32, "a", 4 * P * 4)
    x1nT = place("x1nT", [P, KD, N], F32, "w")
    x1_hi = place("x1_hi", [P, KD, N], F32R, "y")
    x1_lo = place("x1_lo", [P, KD, N], F32R, "y", KD * N * 4)
    t_gu = place("t_gu", [P, 2, 2, D], F32R, "a")
    t_d = place("t_d", [P, 2, D], F32R, "a", 16 * D)
    acc = place("acc", [P, KD, N], F32, "a", 24 * D)
    b4 = CW * 4
    h_hi = place("h_hi", [P, 3, CW], F32R, "xz", 0)
    h_lo = place("h_lo", [P, 3, CW], F32R, "xz", 3 * b4)
    g_acc = place("g_acc", [P, 2, CW], F32, "xz", 6 * b4)
    u_acc = place("u_acc", [P, 2, CW], F32, "xz", 8 * b4)
    u_one = place("u_one", [P, 2, CW], F32, "xz", 10 * b4)
    sg = place("sg", [P, 2, CW], F32, "xz", 12 * b4)
    hh = place("hh", [P, 2, CW], F32, "a", 32512)
    d_one = place("d_one", [P, 2, CW], F32, "a", 32512 + 2 * b4)
    assert 14 * b4 <= at["w"] - at["xz"] and 24 * D + KD * N * 4 <= 32512 and 32512 + 4 * b4 <= NT * N * 4
    assert KD * N * 4 <= at["y"] - at["w"]
    o_sb = place("o_sb", [TP, NT, D], F32, "y")

    ident = small("ident", [P, P], F32)
    ident_b = small("ident_b", [P, P], BF16)
    ones = small("ones", [P, P], F32)
    ones_r = small("ones_r", [P, 2], F32R)
    zeros = small("zeros", [P, P], BF16)
    eps = small("eps", [P, 1], F32)
    iota = small("iota", [P, 512], U16)
    win0 = small("win0", [P, NCP], F32)
    dst_f = small("dst_f", [P, NCP], F32)
    src_hi = small("src_hi", [P, NCP], F32)
    src_lo = small("src_lo", [P, NCP], F32)
    key = small("key", [P, NCP], F32)
    tmp = small("tmp", [P, NCP], F32)
    inside = small("inside", [P, 1], F32)
    flag = small("flag", [P, 1], I32)
    good = small("good", [P, 1], F32)
    bias_b = small("bias_b", [P, D], F32)
    absum = small("absum", [P, 132], F32)
    nscale = small("nscale", [P, 132], F32)
    th_hi = small("th_hi", [P, 132], F32)
    th_lo = small("th_lo", [P, 132], F32)
    bn = small("bn", [P, NT, 6], F32)
    mv = small("mv", [P, NT, 2], F32)
    sd = small("sd", [P, NT], F32)
    rs = small("rs", [P, NT], F32)
    rdeg = small("rdeg", [P, NT], F32)
    ss = small("ss", [P, NT], F32)
    nrm = small("nrm", [P, NT], F32)
    inv = small("inv", [P, NT], F32)
    mv1 = small("mv1", [P, NT, 2], F32)
    sd1 = small("sd1", [P, NT], F32)
    rs1 = small("rs1", [P, NT], F32)
    hot_gen = place("hot_gen", [P, NT * 50], BF16, "hot")
    deg_sum = small("deg_sum", [P, NT], F32)
    blk0 = small("blk0", [P, 25], F32)
    xn = place("xn", [TP, 2, D], F32, "xn")
    junk = place("junk", [TP, D], F32, "raw")

    with ExitStack() as ctx:
        bank = [ctx.enter_context(nc.psum_tensor(f"bank{i}", [P, 512], F32)) for i in range(8)]

        def bf(i):
            return bank[i][:, :].bitcast(BF16)

        def sem(name):
            return ctx.enter_context(nc.semaphore(name))

        const_done = sem("const_done")
        edges_in = sem("edges_in")
        x_in = [sem(f"x_in{t}") for t in range(NT)]
        w_in = sem("w_in")
        raw_in = [sem(f"raw_in{i}") for i in range(RAWS)]
        out_done = sem("out_done")
        prep = sem("prep")
        edges_T = sem("edges_T")
        bn_done = sem("bn_done")
        stats = sem("stats")
        root = sem("root")
        rstd = sem("rstd")
        normed = sem("normed")
        xn_T = sem("xn_T")
        xnT_done = sem("xnT_done")
        y_ready = sem("y_ready")
        z_ready = sem("z_ready")
        yhi_done = sem("yhi_done")
        ylo_done = sem("ylo_done")
        z_done = sem("z_done")
        hot_made = sem("hot_made")
        hot_used = sem("hot_used")
        block_done = sem("block_done")
        block_out = sem("block_out")
        abs_done = sem("abs_done")
        scales = sem("scales")
        above = sem("above")
        ternary = sem("ternary")

        SLOTS = 8 * NT
        FIRST = 6

        def chunks_in(slot):
            def upto(s):
                return 0 if s < FIRST else min(NC, -(-NC * (s - FIRST + 1) // (SLOTS - FIRST)))
            return range(upto(slot - 1), upto(slot))

        def window(c):
            k, off = divmod(STEP * c - LEAD, WIN)
            parts = [(k, off, 0, WIN - off), (k + 1, 0, WIN - off, off)]
            return [p for p in parts if 0 <= p[0] < NB and p[3]]

        first_chunk = [min(c for c in range(NC) if any(p[0] == k for p in window(c))) for k in range(NB)]
        last_chunk = [max(c for c in range(NC) if any(p[0] == k for p in window(c))) for k in range(NB)]

        def blocks_ending(slot):
            return [k for k in range(NB) if last_chunk[k] in chunks_in(slot)]

        loads = []
        for w in (w_gate, w_up):
            for f in range(NF):
                loads.append((w[f * P:(f + 1) * P, :], KD))
        for o in range(KD):
            for f in range(0, NF, 4):
                n = min(4, NF - f)
                loads.append((w_down[o * P:(o + 1) * P, f * P:(f + n) * P], n))
        job_load = [(l, i) for l, (_, n) in enumerate(loads) for i in range(n)]
        JOBS = len(job_load)
        load_end = [sum(n for _, n in loads[:l + 1]) for l in range(len(loads))]
        assert JOBS == 3 * NF * KD

        def tq_of(j):
            if j < 2 * NF * KD:
                return tq_gu[:, j // KD, (j % KD) * P:(j % KD + 1) * P]
            o, f = divmod(j - 2 * NF * KD, NF)
            return tq_d[:, o, f * P:(f + 1) * P]

        def raw_of(j):
            l, i = job_load[j]
            return raw[:, l % RAWS, i * P:(i + 1) * P]

        def jobs_in(slot, lag):
            def upto(s):
                return max(0, min(JOBS, -(-JOBS * (s - lag + 1) // (SLOTS - 6))))
            return range(upto(slot - 1), upto(slot))

        LN_GROUPS = [(0, 1), (1, 4), (4, NT)]

        GB, GC = 50, 32
        GK, GQ = N // GB, NCP // GC
        gen_hot = sem("gen_hot")
        gen_used = sem("gen_used")
        gen_block = sem("gen_block")
        gen_out = sem("gen_out")
        gen_sum = sem("gen_sum")
        gen_taken = sem("gen_taken")

        deg_ready = sem("deg_ready")
        rdeg_done = sem("rdeg_done")
        n_ready = sem("n_ready")
        hsum = sem("hsum")
        leaky = sem("leaky")
        squares = sem("squares")
        norms = sem("norms")
        inv_done = sem("inv_done")
        x1_done = sem("x1_done")
        stats1 = sem("stats1")
        root1 = sem("root1")
        rstd1 = sem("rstd1")
        normed1 = sem("normed1")
        x1n_T = sem("x1n_T")
        x1nT_done = sem("x1nT_done")
        hi_done = sem("hi_done")
        lo_done = sem("lo_done")

        UNITS = [(f, c) for f in range(NF) for c in range(len(CH))]
        NU = len(UNITS)
        LAG = 2
        TURN = ["G0", "U0", "D0", "G1", "U1", "D1", "G2", "U2", "D2", "G3", "U3", "D3"]
        BY_ACT = {"G0", "U0", "U1", "D2", "D3"}
        pieces = []
        for n in range(NU + LAG):
            for what in TURN:
                u = n - LAG if what[0] == "D" else n
                if 0 <= u < NU:
                    pieces.append((u, what))
        index = {p: i for i, p in enumerate(pieces)}
        RING = 7
        took = {}
        for i, (u, what) in enumerate(pieces):
            took[u, what] = 1 + sum((q[1] in BY_ACT) == (what in BY_ACT) for q in pieces[:i])
        piece_ready = sem("piece_ready")
        act_took = sem("act_took")
        dve_took = sem("dve_took")
        u_added = sem("u_added")
        silu_done = sem("silu_done")
        h_done = sem("h_done")
        hhi_done = sem("hhi_done")
        hlo_done = sem("hlo_done")
        d_added = sem("d_added")
        t_ready = sem("t_ready")
        t_done = sem("t_done")
        o_T = sem("o_T")
        o_done = sem("o_done")

        def adds_before(u, what):
            return 2 * (u - 3) + (what == "D3")

        def took_sem(what):
            return act_took if what in BY_ACT else dve_took

        def bank_of(u, what):
            return bank[index[u, what] % RING]

        def general_dve(dve):
            any_outside = dve.value_load(flag[0:1, 0:1])
            with dve.If(any_outside):
                dve.wait_ge(block_out, NB)
                dve.wait_ge(hot_used, NC - 1)
                dve.sem_inc(gen_out, 1)
                dve.sem_inc(gen_taken, 1)
                for sweep in range(2):
                    with dve.Fori(0, GQ) as q:
                        with dve.Fori(0, GK) as k:
                            cs = bass.ds(q * GC, GC)
                            dve.drain()
                            dve.wait_ge(gen_sum, 1 + (sweep * GQ + q) * NT)
                            nc.vector.tensor_scalar(tmp[:, 0:GC], dst_f[:, cs], blk0[:, bass.ds(k, 1)], None, ALU.subtract)
                            dve.drain()
                            nc.vector.tensor_scalar(win0[:, 0:GC], tmp[:, 0:GC], 0.0, None, ALU.is_ge)
                            dve.drain()
                            nc.vector.scalar_tensor_tensor(out=win0[:, 0:GC], in0=tmp[:, 0:GC], scalar=float(GB - 1),
                                                           in1=win0[:, 0:GC], op0=ALU.is_le, op1=ALU.mult)
                            nc.vector.scalar_tensor_tensor(out=key[:, 0:GC], in0=src_hi[:, cs], scalar=float(GB),
                                                           in1=tmp[:, 0:GC], op0=ALU.mult, op1=ALU.add)
                            dve.drain()
                            nc.vector.scalar_tensor_tensor(out=tmp[:, 0:GC], in0=key[:, 0:GC], scalar=1.0, in1=win0[:, 0:GC],
                                                           op0=ALU.add, op1=ALU.mult)
                            dve.drain()
                            nc.vector.tensor_scalar(key[:, 0:GC], tmp[:, 0:GC], 1.0, None, ALU.subtract)
                            dve.drain()
                            nc.vector.tensor_copy(tmp[:, 0:GC], src_lo[:, cs])
                            dve.drain()
                            done = ((sweep * GQ + q) * GK + k) * GC
                            for j in range(GC):
                                dve.wait_ge(gen_used, 1 + done + j)
                                nc.vector.tensor_scalar(hot_src[:, 0, 0:TP], iota[:, 0:TP], tmp[:, j:j + 1], None, ALU.is_equal)
                                nc.vector.tensor_scalar(hot_gen[:, 0:NT * GB], iota[:, 0:NT * GB], key[:, j:j + 1], None,
                                                        ALU.is_equal).then_inc(gen_hot, 1)
                            dve.wait_ge(gen_used, 1 + done + GC)
                            for s in range(NT):
                                last = nc.vector.tensor_scalar(a_t[:, s, bass.ds(k * GB, GB)], bank[7][0:TP, s * GB:(s + 1) * GB],
                                                               1.0, None, ALU.mult)
                            last.then_inc(gen_out, 1)
                        for t in range(NT):
                            dve.wait_ge(gen_sum, 1 + (sweep * GQ + q) * NT + t + 1)
                            if sweep == 0:
                                nc.vector.tensor_copy(tmp[0:TP, 0:1], bank[6][0:TP, 0:1])
                                dve.drain()
                                nc.vector.tensor_tensor(deg_sum[0:TP, t:t + 1], deg_sum[0:TP, t:t + 1], tmp[0:TP, 0:1],
                                                        ALU.add).then_inc(gen_taken, 1)
                            else:
                                nc.vector.scalar_tensor_tensor(out=z[:, t, :], in0=bank[6][0:TP, :], scalar=deg_sum[0:TP, t:t + 1],
                                                               in1=z[:, t, :], op0=ALU.mult, op1=ALU.add).then_inc(gen_taken, 1)
                    if sweep == 0:
                        dve.drain()
                        nc.vector.tensor_scalar(rdeg[0:TP, :], deg_sum[0:TP, :], 1.0, None, ALU.max)
                        dve.drain()
                        nc.vector.reciprocal(deg_sum[0:TP, :], rdeg[0:TP, :])
                        dve.drain()

        def general_pe(pe):
            any_outside = pe.value_load(flag[0:1, 0:1])
            with pe.If(any_outside):
                pe.wait_ge(z_done, NT)
                pe.wait_ge(ylo_done, NT)
                pe.sem_inc(gen_used, 1)
                pe.sem_inc(gen_sum, 1)
                for sweep in range(2):
                    with pe.Fori(0, GQ) as q:
                        with pe.Fori(0, GK) as k:
                            done = ((sweep * GQ + q) * GK + k) * GC
                            pe.wait_ge(gen_out, 1 + (sweep * GQ + q) * GK + k)
                            for j in range(GC):
                                pe.wait_ge(gen_hot, done + j + 1)
                                nc.tensor.matmul(bank[7][0:TP, 0:NT * GB], hot_src[:, 0, 0:TP], hot_gen[:, 0:NT * GB],
                                                 start=j == 0, stop=j == GC - 1).then_inc(gen_used, 1)
                        pe.wait_ge(gen_out, 1 + (sweep * GQ + q + 1) * GK)
                        for t in range(NT):
                            pe.wait_ge(gen_taken, 1 + (sweep * GQ + q) * NT + t)
                            if sweep == 0:
                                for s in range(NT):
                                    last = nc.tensor.matmul(bank[6][0:TP, 0:2], a_t[:, s, t * TP:(t + 1) * TP], ones_r[0:TP, :],
                                                            start=s == 0, stop=s == NT - 1)
                            else:
                                for s in range(NT):
                                    for y in (y_hi, y_lo):
                                        last = nc.tensor.matmul(bank[6][0:TP, :], a_t[:, s, t * TP:(t + 1) * TP], y[:, s, :],
                                                                start=s == 0 and y is y_hi, stop=s == NT - 1 and y is y_lo)
                            last.then_inc(gen_sum, 1)

        block = ctx.enter_context(nc.Block())

        @block.sync
        def _(sp):
            sp.wait_ge(const_done, 1)
            for i, v in enumerate((src, dst)):
                sp.dma_start(e_i[:, 2 * i, :], v[0:P * P].rearrange("(c e) -> c e", e=P)).then_inc(edges_in, 16)
                n = E // P - P
                sp.dma_start(e_i[0:n, 2 * i + 1, :], v[P * P:(P + n) * P].rearrange("(c e) -> c e", e=P)).then_inc(edges_in, 16)
                sp.dma_start(e_i[n:n + 1, 2 * i + 1, 0:E - (P + n) * P],
                             v[(P + n) * P:E].rearrange("(c e) -> c e", c=1)).then_inc(edges_in, 16)
            for t in range(NT):
                sp.dma_start(x_sb[0:112, t, :], x[t * TP:t * TP + 112, :]).then_inc(x_in[t], 16)
                sp.dma_start(x_sb[112:TP, t, :], x[t * TP + 112:(t + 1) * TP, :]).then_inc(x_in[t], 16)
                if t == 0:
                    sp.dma_start(w_sb[:, :, 0:D], w_neigh.rearrange("(k p) n -> p k n", p=P)).then_inc(w_in, 16)
                    sp.dma_start(w_sb[:, :, D:2 * D], w_self.rearrange("(k p) n -> p k n", p=P)).then_inc(w_in, 16)
                    sp.dma_start(bias_b[:, :], bias.rearrange("(a n) -> a n", a=1).to_broadcast([P, D])).then_inc(w_in, 16)
            for l, (w, n) in enumerate(loads):
                if l >= RAWS:
                    sp.wait_ge(ternary, load_end[l - RAWS])
                sp.dma_start(raw[:, l % RAWS, 0:n * P], w).then_inc(raw_in[l % RAWS], 16)
            for t in range(NT):
                sp.wait_ge(o_done, t + 1)
                sp.dma_start(out[t * TP:t * TP + 112, :], o_sb[0:112, t, :]).then_inc(out_done, 16)
                sp.dma_start(out[t * TP + 112:(t + 1) * TP, :], o_sb[112:TP, t, :]).then_inc(out_done, 16)
            sp.wait_ge(out_done, 32 * NT)

        @block.gpsimd
        def _(pool):
            nc.gpsimd.memset(e_i[:], -1).then_inc(const_done, 1)
            nc.gpsimd.memset(ident[:], 1.0).then_inc(const_done, 1)
            nc.gpsimd.memset(ident_b[:], 1.0).then_inc(const_done, 1)
            pool.wait_ge(const_done, 3)
            for m in (ident, ident_b):
                nc.gpsimd.affine_select(out=m[:], in_=m[:], compare_op=ALU.is_equal, fill=0.0, base=0,
                                        pattern=[[-1, P]], channel_multiplier=1).then_inc(const_done, 1)
            nc.gpsimd.iota(win0[:], pattern=[[STEP, NCP]], base=-LEAD, channel_multiplier=0,
                           allow_small_or_imprecise_dtypes=True).then_inc(const_done, 1)
            nc.gpsimd.iota(iota[:], pattern=[[1, 512]], base=0, channel_multiplier=0,
                           allow_small_or_imprecise_dtypes=True).then_inc(const_done, 1)
            nc.gpsimd.iota(blk0[:], pattern=[[GB, GK]], base=0, channel_multiplier=0,
                           allow_small_or_imprecise_dtypes=True).then_inc(const_done, 1)
            nc.gpsimd.memset(ones[:], 1.0).then_inc(const_done, 1)
            nc.gpsimd.memset(zeros[:], 0.0).then_inc(const_done, 1)
            nc.gpsimd.memset(eps[:], LN_EPS).then_inc(const_done, 1)
            nc.gpsimd.memset(deg_sum[:], 0.0).then_inc(const_done, 1)
            step = 0
            for l, (_, n) in enumerate(loads):
                js = slice(load_end[l] - n, load_end[l])
                pool.wait_ge(abs_done, load_end[l])
                nc.gpsimd.tensor_scalar(nscale[:, js], absum[:, js], -1.0 / P, -Q_EPS, ALU.mult, ALU.add).then_inc(scales, 1)
                step += 1
                pool.wait_ge(scales, step)
                nc.gpsimd.tensor_scalar(th_hi[:, js], nscale[:, js], -0.5, 0.0, ALU.mult, ALU.add).then_inc(scales, 1)
                nc.gpsimd.tensor_scalar(th_lo[:, js], nscale[:, js], 0.5, 0.0, ALU.mult, ALU.add).then_inc(scales, 1)
                step += 2
                pool.wait_ge(scales, step)
                for j in range(js.start, js.stop):
                    nc.gpsimd.tensor_scalar(tq_of(j), raw_of(j), th_hi[:, j:j + 1], None, ALU.is_gt).then_inc(above, 1)

            def add_down(u, what):
                f, c = UNITS[u]
                s0, n = CH[c]
                o = int(what[1])
                if f == 0:
                    return 0
                pool.wait_ge(act_took, took[u, what])
                if f > 1:
                    pool.wait_ge(d_added, adds_before(u - 3, what) + 1)
                to = acc[:, o, s0:s0 + n]
                nc.gpsimd.tensor_tensor(to, to, d_one[:, o - 2, 0:n], ALU.add).then_inc(d_added, 1)

            for n in range(NU + LAG):
                if n < NU:
                    w = CH[UNITS[n][1]][1]
                    pool.wait_ge(act_took, took[n, "U1"])
                    to = u_acc[:, n % 2, 0:w]
                    nc.gpsimd.tensor_tensor(to, to, u_one[:, n % 2, 0:w], ALU.add).then_inc(u_added, 1)
                if 1 <= n <= NU:
                    u = n - 1
                    w = CH[UNITS[u][1]][1]
                    pool.wait_ge(silu_done, u + 1)
                    pool.wait_ge(dve_took, took[u, "U3"])
                    if u >= 2:
                        pool.wait_ge(hlo_done, u - 1)
                    nc.gpsimd.tensor_tensor(hh[:, u % 2, 0:w], sg[:, u % 2, 0:w], u_acc[:, u % 2, 0:w], ALU.mult).then_inc(h_done, 1)
                if n >= LAG:
                    add_down(n - LAG, "D2")
                    add_down(n - LAG, "D3")

        @block.scalar
        def _(act):
            def layernorm_root(g, ready, var, sdev, done):
                a, b = g
                act.wait_ge(ready, b)
                nc.scalar.activation(sdev[0:TP, a:b], var[0:TP, a:b, 1], ACT.Sqrt, bias=eps[0:TP, :]).then_inc(done, 1)

            act.wait_ge(const_done, 12)
            for slot in range(SLOTS + 8):
                t, i = divmod(slot, 8)
                if slot == 0:
                    layernorm_root(LN_GROUPS[0], stats, mv, sd, root)
                    act.wait_ge(xn_T, 1)
                    nc.scalar.activation(xnT[:, 0, 0:KD * TP], bank[3][:, 0:KD * TP], ACT.Copy).then_inc(xnT_done, 1)
                    layernorm_root(LN_GROUPS[1], stats, mv, sd, root)
                if slot == 4:
                    layernorm_root(LN_GROUPS[2], stats, mv, sd, root)
                if i == 1 and 1 <= t <= NT:
                    act.wait_ge(y_ready, t)
                    nc.scalar.activation(y_hi[:, t - 1, :], bank[4 + (t - 1) % 2][0:TP, :], ACT.Copy).then_inc(yhi_done, 1)
                if i == 5 and t + 1 < NT:
                    act.wait_ge(xn_T, t + 2)
                    nc.scalar.activation(xnT[:, t + 1, 0:KD * TP], bank[3][:, 0:KD * TP], ACT.Copy).then_inc(xnT_done, 1)
                if slot < SLOTS:
                    for j in jobs_in(slot, 0):
                        l, _ = job_load[j]
                        act.wait_ge(raw_in[l % RAWS], 16 * (l // RAWS + 1))
                        nc.scalar.activation(tq_of(j), raw_of(j), ACT.Abs, accum_out=absum[:, j:j + 1]).then_inc(abs_done, 1)
                    for k in blocks_ending(slot):
                        act.wait_ge(block_done, k + 1)
                        n = min(WIN, N - k * WIN)
                        nc.scalar.activation(
                            a_t[:, :, k * WIN:k * WIN + n],
                            bank[k % 3][0:TP, 0:NT * WIN].rearrange("p (s d) -> p s d", d=WIN)[:, :, 0:n],
                            ACT.Copy).then_inc(block_out, 1)
            for n in range(NT + 4):
                if n < NT:
                    act.wait_ge(leaky, n + 1)
                    if n >= 1:
                        act.wait_ge(squares, n)
                    nc.scalar.activation(junk[:], z[:, n, :], ACT.Square, accum_out=ss[0:TP, n:n + 1]).then_inc(squares, 1)
                    act.wait_ge(squares, n + 1)
                    nc.scalar.activation(nrm[0:TP, n:n + 1], ss[0:TP, n:n + 1], ACT.Sqrt).then_inc(norms, 1)
                if 1 <= n <= NT:
                    act.wait_ge(stats1, n)
                    nc.scalar.activation(sd1[0:TP, n - 1:n], mv1[0:TP, n - 1:n, 1], ACT.Sqrt, bias=eps[0:TP, :]).then_inc(root1, 1)
                if 3 <= n < NT + 3:
                    t = n - 3
                    act.wait_ge(x1n_T, t + 1)
                    nc.scalar.activation(x1nT[:, :, t * TP:(t + 1) * TP],
                                         bank[4 + t % 2][:, 0:KD * TP].rearrange("p (k s) -> p k s", k=KD),
                                         ACT.Copy).then_inc(x1nT_done, 1)

            def ternary_out(f, down):
                act.wait_ge(t_ready, 2 * f + 1 + down)
                if not down:
                    if f >= 2:
                        act.wait_ge(piece_ready, index[3 * (f - 2) + 2, "U3"] + 1)
                    nc.scalar.activation(t_gu[:, f % 2, :, :].rearrange("p a d -> p (a d)"), bf(7)[:, 0:2 * D],
                                         ACT.Copy).then_inc(t_done, 1)
                else:
                    if f >= 2:
                        act.wait_ge(piece_ready, index[3 * (f - 2) + 2, "D3"] + 1)
                    nc.scalar.activation(t_d[:, f % 2, :], bf(7)[:, 0:D], ACT.Copy).then_inc(t_done, 1)

            act.wait_ge(n_ready, NT)
            ternary_out(0, 0)
            for c, (s0, n) in enumerate(CH):
                act.wait_ge(x1nT_done, NT)
                nc.scalar.activation(x1_hi[:, :, s0:s0 + n], x1nT[:, :, s0:s0 + n], ACT.Copy).then_inc(hi_done, 1)
            ternary_out(0, 1)

            def take(u, what, to):
                f, c = UNITS[u]
                n = CH[c][1]
                k = int(what[1])
                j = {"G": 4 * f + k, "U": 4 * NF + 4 * f + k, "D": 8 * NF + NF * k + f}[what[0]]
                act.wait_ge(piece_ready, index[u, what] + 1)
                nc.scalar.activation(to, bank_of(u, what)[:, 0:n], ACT.Copy, scale=nscale[:, j:j + 1]).then_inc(act_took, 1)

            for n in range(NU + LAG):
                f, c = UNITS[n] if n < NU else (NF, 0)
                if n < NU:
                    w = CH[c][1]
                    if n >= 2:
                        act.wait_ge(silu_done, n - 1)
                    take(n, "G0", g_acc[:, n % 2, 0:w])
                    if n >= 2:
                        act.wait_ge(h_done, n - 1)
                    take(n, "U0", u_acc[:, n % 2, 0:w])
                if 1 <= n <= NU:
                    u = n - 1
                    wu = CH[UNITS[u][1]][1]
                    act.wait_ge(dve_took, took[u, "G3"])
                    nc.scalar.activation(sg[:, u % 2, 0:wu], g_acc[:, u % 2, 0:wu], ACT.Silu).then_inc(silu_done, 1)
                if n < NU:
                    if n >= 2:
                        act.wait_ge(u_added, n - 1)
                    take(n, "U1", u_one[:, n % 2, 0:w])
                for what in ("D2", "D3"):
                    if what == "D3" and 1 <= n <= NU:
                        act.wait_ge(h_done, u + 1)
                        if u >= 3:
                            act.wait_ge(piece_ready, index[u - 3, "D3"] + 1)
                        nc.scalar.activation(h_hi[:, u % 3, 0:wu], hh[:, u % 2, 0:wu], ACT.Copy).then_inc(hhi_done, 1)
                    if n >= LAG:
                        v = n - LAG
                        fv, cv = UNITS[v]
                        s0, wv = CH[cv]
                        if fv == 0:
                            take(v, what, acc[:, int(what[1]), s0:s0 + wv])
                        else:
                            if adds_before(v, what) >= 2:
                                act.wait_ge(d_added, adds_before(v, what) - 1)
                            take(v, what, d_one[:, int(what[1]) - 2, 0:wv])
                if n < NU and f + 1 < NF:
                    if c == 0:
                        ternary_out(f + 1, 0)
                    if c == 2:
                        ternary_out(f + 1, 1)

        @block.vector
        def _(dve):
            steps = [0]

            def link(ins):
                steps[0] += 1
                ins.then_inc(prep, 1)
                dve.wait_ge(prep, steps[0])

            def normalize(t):
                if t >= 2:
                    dve.wait_ge(xn_T, t - 1)
                nc.vector.tensor_scalar(xn[:, t % 2, :], x_sb[:, t, :], mv[0:TP, t, 0:1], rs[0:TP, t:t + 1],
                                        ALU.subtract, ALU.mult).then_inc(normed, 1)

            def statistics(g):
                for t in range(*g):
                    dve.wait_ge(x_in[t], 32)
                    nc.vector.bn_stats(bn[0:TP, t, :], x_sb[:, t, :]).then_inc(bn_done, 1)
                for t in range(*g):
                    dve.wait_ge(bn_done, t + 1)
                    nc.vector.bn_aggr(mv[0:TP, t, :], bn[0:TP, t, :]).then_inc(stats, 1)

            def reciprocals(i):
                a, b = LN_GROUPS[i]
                dve.wait_ge(root, i + 1)
                nc.vector.reciprocal(rs[0:TP, a:b], sd[0:TP, a:b]).then_inc(rstd, 1)
                dve.wait_ge(rstd, i + 1)

            dve.wait_ge(const_done, 12)
            nc.vector.tensor_copy(ones_r[:], ones[:, 0:2]).then_inc(prep, 1)
            steps[0] += 1
            dve.wait_ge(edges_in, 96)
            link(nc.vector.tensor_copy(e_f[:], e_i[:]))
            statistics(LN_GROUPS[0])
            reciprocals(0)
            normalize(0)
            dve.wait_ge(edges_T, 1)
            srcs, dsts = bank[5][:, 0:NCP], bank[5][:, NCP:2 * NCP]
            nc.vector.tensor_copy(dst_f[:], dsts).then_inc(prep, 1)
            steps[0] += 1
            link(nc.vector.tensor_scalar(tmp[:], srcs, (TP - 1) / 2, 1.0 / TP, ALU.subtract, ALU.mult))
            link(nc.vector.tensor_scalar(src_hi[:], tmp[:], ROUND, ROUND, ALU.add, ALU.subtract))
            link(nc.vector.scalar_tensor_tensor(out=src_lo[:], in0=src_hi[:], scalar=-float(TP), in1=srcs, op0=ALU.mult, op1=ALU.add))
            link(nc.vector.tensor_tensor(tmp[:], dst_f[:], win0[:], ALU.subtract))
            link(nc.vector.tensor_scalar(key[:], tmp[:], 0.0, None, ALU.is_ge))
            link(nc.vector.scalar_tensor_tensor(out=win0[:], in0=tmp[:], scalar=float(WIN - 1), in1=key[:], op0=ALU.is_le,
                                                op1=ALU.mult, accum_out=inside[:]))
            link(nc.vector.scalar_tensor_tensor(out=key[:], in0=src_hi[:], scalar=float(WIN), in1=tmp[:], op0=ALU.mult, op1=ALU.add))
            link(nc.vector.scalar_tensor_tensor(out=tmp[:], in0=key[:], scalar=1.0, in1=win0[:], op0=ALU.add, op1=ALU.mult))
            link(nc.vector.tensor_scalar(key[:], tmp[:], 1.0, None, ALU.subtract))
            statistics(LN_GROUPS[1])
            reciprocals(1)
            normalize(1)
            dve.wait_ge(edges_T, 2)
            nc.vector.tensor_scalar(good[:], bank[6][:, 0:1], float(E), None, ALU.is_equal).then_inc(prep, 1)
            nc.vector.tensor_scalar(flag[:], bank[6][:, 0:1], float(E), None, ALU.is_lt).then_inc(prep, 1)
            steps[0] += 2

            for slot in range(SLOTS + 8):
                t, i = divmod(slot, 8)
                if slot == 3:
                    statistics(LN_GROUPS[2])
                if slot == 5:
                    reciprocals(2)
                if i == 0 and 1 <= t and t + 1 < NT:
                    normalize(t + 1)
                if i == 2 and 1 <= t <= NT:
                    dve.wait_ge(yhi_done, t)
                    nc.vector.tensor_tensor(y_lo[:, t - 1, :], bank[4 + (t - 1) % 2][0:TP, :],
                                            y_hi[:, t - 1, :].bitcast(F32), ALU.subtract).then_inc(ylo_done, 1)
                if i == 3 and 1 <= t <= NT:
                    dve.wait_ge(z_ready, t)
                    if t == 1:
                        dve.wait_ge(w_in, 48)
                    nc.vector.tensor_tensor(z[:, t - 1, :], bank[6 + (t - 1) % 2][0:TP, :], bias_b[0:TP, :],
                                            ALU.add).then_inc(z_done, 1)
                if slot < SLOTS:
                    for c in chunks_in(slot):
                        if c >= HOT:
                            dve.wait_ge(hot_used, c - HOT + 1)
                        nc.vector.tensor_scalar(hot_src[:, c % HOT, 0:TP], iota[:, 0:TP], src_lo[:, c:c + 1], None, ALU.is_equal)
                        nc.vector.tensor_scalar(hot_dst[:, c % HOT, :], iota[:, 0:NT * WIN], key[:, c:c + 1], None,
                                                ALU.is_equal).then_inc(hot_made, 1)
                for j in jobs_in(slot, 4):
                    dve.wait_ge(above, j + 1)
                    nc.vector.scalar_tensor_tensor(out=tq_of(j), in0=raw_of(j), scalar=th_lo[:, j:j + 1], in1=tq_of(j),
                                                   op0=ALU.is_lt, op1=ALU.subtract).then_inc(ternary, 1)

            general_dve(dve)

            dve.wait_ge(deg_ready, 1)
            nc.vector.tensor_scalar(rdeg[0:TP, :], bank[2][0:TP, 0:2 * NT].rearrange("p (t a) -> p t a", a=2)[:, :, 0],
                                    1.0, None, ALU.max).then_inc(rdeg_done, 1)
            dve.wait_ge(rdeg_done, 1)
            nc.vector.reciprocal(rs[0:TP, :], rdeg[0:TP, :]).then_inc(rdeg_done, 1)
            dve.wait_ge(rdeg_done, 2)
            nc.vector.tensor_scalar(rdeg[0:TP, :], rs[0:TP, :], good[0:TP, :], None, ALU.mult).then_inc(rdeg_done, 1)
            dve.wait_ge(rdeg_done, 3)
            for n in range(NT + 2):
                if n < NT:
                    dve.wait_ge(n_ready, n + 1)
                    nc.vector.scalar_tensor_tensor(out=z[:, n, :], in0=bank[n % 2][0:TP, :], scalar=rdeg[0:TP, n:n + 1],
                                                   in1=z[:, n, :], op0=ALU.mult, op1=ALU.add).then_inc(hsum, 1)
                if 1 <= n <= NT:
                    t = n - 1
                    dve.wait_ge(norms, t + 1)
                    nc.vector.tensor_scalar(nrm[0:TP, t:t + 1], nrm[0:TP, t:t + 1], NORM_EPS, None, ALU.max).then_inc(inv_done, 1)
                    dve.wait_ge(inv_done, 2 * t + 1)
                    nc.vector.reciprocal(inv[0:TP, t:t + 1], nrm[0:TP, t:t + 1]).then_inc(inv_done, 1)
                    if n < NT:
                        dve.wait_ge(hsum, n + 1)
                        nc.vector.scalar_tensor_tensor(out=z[:, n, :], in0=z[:, n, :], scalar=SLOPE, in1=z[:, n, :],
                                                       op0=ALU.mult, op1=ALU.max).then_inc(leaky, 1)
                    dve.wait_ge(inv_done, 2 * t + 2)
                    nc.vector.scalar_tensor_tensor(out=x_sb[:, t, :], in0=z[:, t, :], scalar=inv[0:TP, t:t + 1],
                                                   in1=x_sb[:, t, :], op0=ALU.mult, op1=ALU.add).then_inc(x1_done, 1)
                elif n < NT:
                    dve.wait_ge(hsum, n + 1)
                    nc.vector.scalar_tensor_tensor(out=z[:, n, :], in0=z[:, n, :], scalar=SLOPE, in1=z[:, n, :],
                                                   op0=ALU.mult, op1=ALU.max).then_inc(leaky, 1)
                if 2 <= n:
                    t = n - 2
                    dve.wait_ge(root1, t + 1)
                    nc.vector.reciprocal(rs1[0:TP, t:t + 1], sd1[0:TP, t:t + 1]).then_inc(rstd1, 1)
                if 1 <= n <= NT:
                    t = n - 1
                    dve.wait_ge(x1_done, t + 1)
                    nc.vector.bn_stats(bn[0:TP, t, :], x_sb[:, t, :]).then_inc(bn_done, 1)
                    dve.wait_ge(bn_done, NT + t + 1)
                    nc.vector.bn_aggr(mv1[0:TP, t, :], bn[0:TP, t, :]).then_inc(stats1, 1)
                if 2 <= n:
                    t = n - 2
                    dve.wait_ge(rstd1, t + 1)
                    if t >= 2:
                        dve.wait_ge(x1n_T, t - 1)
                    nc.vector.tensor_scalar(xn[:, t % 2, :], x_sb[:, t, :], mv1[0:TP, t, 0:1], rs1[0:TP, t:t + 1],
                                            ALU.subtract, ALU.mult).then_inc(normed1, 1)
            for c, (s0, n) in enumerate(CH):
                dve.wait_ge(hi_done, c + 1)
                nc.vector.tensor_tensor(x1_lo[:, :, s0:s0 + n], x1nT[:, :, s0:s0 + n], x1_hi[:, :, s0:s0 + n].bitcast(F32),
                                        ALU.subtract).then_inc(lo_done, 1)

            def take(u, what):
                f, c = UNITS[u]
                s0, n = CH[c]
                k = int(what[1])
                j = {"G": 4 * f + k, "U": 4 * NF + 4 * f + k, "D": 8 * NF + NF * k + f}[what[0]]
                to = {"G": g_acc[:, u % 2, 0:n], "U": u_acc[:, u % 2, 0:n], "D": acc[:, k, s0:s0 + n]}[what[0]]
                dve.wait_ge(piece_ready, index[u, what] + 1)
                if what == "G1":
                    dve.wait_ge(act_took, took[u, "G0"])
                elif what == "U2":
                    dve.wait_ge(u_added, u + 1)
                elif what[0] != "D":
                    dve.wait_ge(dve_took, took[u, what[0] + str(k - 1)])
                elif f:
                    dve.wait_ge(dve_took, took[u - 3, what])
                if what[0] == "D" and f == 0:
                    nc.vector.tensor_scalar(to, bank_of(u, what)[:, 0:n], nscale[:, j:j + 1], None, ALU.mult).then_inc(dve_took, 1)
                else:
                    nc.vector.scalar_tensor_tensor(out=to, in0=bank_of(u, what)[:, 0:n], scalar=nscale[:, j:j + 1], in1=to,
                                                   op0=ALU.mult, op1=ALU.add).then_inc(dve_took, 1)

            for n in range(NU + LAG):
                for what in TURN:
                    u = n - LAG if what[0] == "D" else n
                    if 0 <= u < NU and what not in BY_ACT:
                        take(u, what)
                if 1 <= n <= NU:
                    u = n - 1
                    w = CH[UNITS[u][1]][1]
                    dve.wait_ge(hhi_done, u + 1)
                    nc.vector.tensor_tensor(h_lo[:, u % 3, 0:w], hh[:, u % 2, 0:w], h_hi[:, u % 3, 0:w].bitcast(F32),
                                            ALU.subtract).then_inc(hlo_done, 1)
            for t in range(NT):
                dve.wait_ge(o_T, t + 1)
                nc.vector.tensor_tensor(o_sb[:, t, :], bank[t % 4][0:TP, :], x_sb[:, t, :], ALU.add).then_inc(o_done, 1)

        @block.tensor
        def _(pe):
            def transpose_xn(t, ready, to, done):
                pe.wait_ge(ready, t + 1)
                for k in range(KD):
                    last = nc.tensor.transpose(to[:, k * TP:(k + 1) * TP], xn[:, t % 2, k * P:(k + 1) * P], ident[0:TP, 0:TP])
                last.then_inc(done, 1)

            def add_chunk(c):
                pe.wait_ge(hot_made, c + 1)
                parts = window(c)
                for k, d0, w0, n in parts:
                    if c == first_chunk[k] and k >= 3:
                        pe.wait_ge(block_out, k - 2)
                    last = nc.tensor.matmul(
                        bank[k % 3][0:TP, 0:NT * WIN].rearrange("p (s d) -> p s d", d=WIN)[:, :, d0:d0 + n],
                        hot_src[:, c % HOT, 0:TP],
                        hot_dst[:, c % HOT, :].rearrange("p (s d) -> p s d", d=WIN)[:, :, w0:w0 + n],
                        start=c == first_chunk[k], stop=c == last_chunk[k], skip_group_check=True)
                    if c == last_chunk[k]:
                        last.then_inc(block_done, 1)
                    elif (k, d0, w0, n) == parts[-1]:
                        last.then_inc(hot_used, 1)

            pe.wait_ge(const_done, 12)
            pe.wait_ge(prep, 2)
            for i, (rows, col) in enumerate(((P, 0), (32, P), (P, NCP), (32, NCP + P))):
                last = nc.tensor.transpose(bank[5][:, col:col + rows], e_f[0:rows, i, :], ident[0:rows, 0:rows])
            last.then_inc(edges_T, 1)
            transpose_xn(0, normed, bank[3], xn_T)
            for slot in range(SLOTS):
                t, i = divmod(slot, 8)
                if i == 0:
                    pe.wait_ge(xnT_done, t + 1)
                    if t == 0:
                        pe.wait_ge(w_in, 48)
                    if t >= 2:
                        pe.wait_ge(ylo_done, t - 1)
                if i == 4 and t >= 2:
                    pe.wait_ge(z_done, t - 1)
                if slot == 4:
                    pe.wait_ge(prep, 9)
                    nc.tensor.matmul(bank[6][:, 0:1], ones[:], inside[:], start=True, stop=True).then_inc(edges_T, 1)
                    pe.wait_ge(prep, 14)
                k, half = i % 4, i // 4
                to = bank[(6 if half else 4) + t % 2]
                last = nc.tensor.matmul(to[0:TP, :], xnT[:, t, k * TP:(k + 1) * TP], w_sb[:, k, half * D:(half + 1) * D],
                                        start=k == 0, stop=k == KD - 1)
                if k == KD - 1:
                    last.then_inc(z_ready if half else y_ready, 1)
                if i == 4 and t + 1 < NT:
                    transpose_xn(t + 1, normed, bank[3], xn_T)
                for c in chunks_in(slot):
                    add_chunk(c)

            general_pe(pe)

            pe.wait_ge(block_out, NB)
            pe.wait_ge(prep, 1)
            for t in range(NT):
                for s in range(NT):
                    last = nc.tensor.matmul(bank[2][0:TP, 2 * t:2 * t + 2], a_t[:, s, t * TP:(t + 1) * TP], ones_r[0:TP, :],
                                            start=s == 0, stop=s == NT - 1, skip_group_check=True)
            last.then_inc(deg_ready, 1)
            pe.wait_ge(ylo_done, NT)
            for n in range(NT + 3):
                if n < NT:
                    if n >= 2:
                        pe.wait_ge(hsum, n - 1)
                    for s in range(NT):
                        for y in (y_hi, y_lo):
                            last = nc.tensor.matmul(bank[n % 2][0:TP, :], a_t[:, s, n * TP:(n + 1) * TP], y[:, s, :],
                                                    start=s == 0 and y is y_hi, stop=s == NT - 1 and y is y_lo)
                    last.then_inc(n_ready, 1)
                if 3 <= n:
                    t = n - 3
                    if t >= 2:
                        pe.wait_ge(x1nT_done, t - 1)
                    if t == 0:
                        pe.wait_ge(z_done, NT)
                    transpose_xn(t, normed1, bank[4 + t % 2], x1n_T)

            def ternary_in(f, down):
                pe.wait_ge(ternary, JOBS)
                if 2 * f + down:
                    pe.wait_ge(t_done, 2 * f + down)
                if not down:
                    for a in range(2):
                        for k in range(KD):
                            last = nc.tensor.transpose(bf(7)[:, a * D + k * P:a * D + (k + 1) * P],
                                                       tq_gu[:, a * NF + f, k * P:(k + 1) * P], ident_b[:])
                else:
                    for o in range(KD):
                        last = nc.tensor.transpose(bf(7)[:, o * P:(o + 1) * P], tq_d[:, o, f * P:(f + 1) * P], ident_b[:])
                last.then_inc(t_ready, 1)

            ternary_in(0, 0)
            ternary_in(0, 1)
            pe.wait_ge(x1nT_done, NT)
            for i, (u, what) in enumerate(pieces):
                f, c = UNITS[u]
                s0, n = CH[c]
                k = int(what[1])
                if what == "G0":
                    if u < 3:
                        pe.wait_ge(lo_done, u + 1)
                    if c == 0:
                        pe.wait_ge(t_done, 2 * f + 1)
                if what == "D0":
                    pe.wait_ge(hlo_done, u + 1)
                    if c == 0:
                        pe.wait_ge(t_done, 2 * f + 2)
                if i >= RING:
                    old = pieces[i - RING]
                    pe.wait_ge(took_sem(old[1]), took[old])
                if what[0] == "D":
                    w = t_d[:, f % 2, k * P:(k + 1) * P]
                    parts = (h_hi[:, u % 3, 0:n], h_lo[:, u % 3, 0:n])
                else:
                    w = t_gu[:, f % 2, int(what[0] == "U"), k * P:(k + 1) * P]
                    parts = (x1_hi[:, k, s0:s0 + n], x1_lo[:, k, s0:s0 + n])
                for h in range(2):
                    last = nc.tensor.matmul(bank_of(u, what)[:, 0:n], w, parts[h], start=h == 0, stop=h == 1)
                last.then_inc(piece_ready, 1)
                if what == "U3" and f + 1 < NF:
                    if c == 0:
                        ternary_in(f + 1, 0)
                    if c == 2:
                        ternary_in(f + 1, 1)
            pe.wait_ge(dve_took, took[pieces[-2][0], "D1"])
            pe.wait_ge(act_took, took[pieces[-1]])
            for t in range(NT):
                for u in range(NU - 3, NU):
                    s0, n = CH[UNITS[u][1]]
                    if s0 < (t + 1) * TP and t * TP < s0 + n:
                        pe.wait_ge(d_added, adds_before(u, "D3") + 1)
                if t >= 4:
                    pe.wait_ge(o_done, t - 3)
                for k in range(KD):
                    last = nc.tensor.transpose(bank[t % 4][0:TP, k * P:(k + 1) * P], acc[:, k, t * TP:(t + 1) * TP], ident[:])
                last.then_inc(o_T, 1)


_INS = ["x", "src", "dst", "L0_gnn_W_self", "L0_gnn_W_neigh", "L0_gnn_b", "L0_ffn_w_gate", "L0_ffn_w_up", "L0_ffn_w_down"]


def kernel(**inputs):
    import numpy as np
    import concourse.bacc as bacc
    from concourse.bass_utils import run_bass_kernel_spmd

    nc = bacc.Bacc("TRN2", target_bir_lowering=False, num_devices=1)
    arrays, args = {}, []
    for name in _INS:
        a = np.ascontiguousarray(inputs[name])
        arrays[f"in_{name}"] = a
        args.append(nc.dram_tensor(f"in_{name}", a.shape, mybir.dt.from_np(a.dtype), kind="ExternalInput").ap())
    shape = arrays["in_x"].shape
    args.append(nc.dram_tensor("out_x", shape, F32, kind="ExternalOutput").ap())
    gnn_ffn(nc, *args)
    r = run_bass_kernel_spmd(nc, [arrays], core_ids=[0])
    return r.results[0]["out_x"]
```

```python
from contextlib import ExitStack

import concourse.bass as bass
from concourse import mybir

F32 = mybir.dt.float32
F32R = mybir.dt.float32r
BF16 = mybir.dt.bfloat16
U16 = mybir.dt.uint16
I32 = mybir.dt.int32
ALU = mybir.AluOpType
ACT = mybir.ActivationFunctionType

P = 128
WIN = 48
ROUND = 12582912.0
LN_EPS = 1e-5
NORM_EPS = 1e-12
Q_EPS = 1e-5
SLOPE = 0.01


def gnn_ffn(nc, x, src, dst, w_self, w_neigh, bias, w_gate, w_up, w_down, out):
    N, D = x.shape
    E = src.shape[0]
    F = w_gate.shape[0]
    TP = 125
    NT = N // TP
    KD = D // P
    NF = F // P
    NC = -(-E // P)
    NCP = 160
    EPD = E // N
    STEP = P // EPD
    LEAD = (WIN - STEP) // 2
    NB = -(-N // WIN)
    assert (N, D, E, F) == (TP * NT, 512, EPD * N, 1408) and NC == 157 and WIN % STEP == 0

    HOT = 4
    RW = 4 * P
    RAWS = 4
    CH = [(0, 418), (418, 416), (834, 416)]
    CW = 424

    base = 17408
    at = {}
    for name, size in (
        ("x", NT * D * 4), ("tq_gu", 2 * NF * D * 2), ("tq_d", KD * F * 2), ("xz", NT * D * 4), ("raw", RAWS * RW * 4),
        ("w", KD * 2 * D * 4), ("hot", HOT * (NT * WIN + P) * 2), ("y", 2 * NT * D * 4), ("a", NT * N * 4),
        ("xn", 2 * D * 4), ("small", 12288),
    ):
        at[name] = base
        base += -(-size // 32) * 32
    assert base <= 229368, base
    used = {"small": 0}

    def place(name, shape, dt, region, offset=0):
        return nc.alloc_sbuf_tensor_at(name, shape, dt, offset=at[region] + offset)

    def small(name, shape, dt):
        width = {F32: 4, F32R: 4, I32: 4, BF16: 2, U16: 2}[dt]
        for n in shape[1:]:
            width *= n
        o = used["small"]
        used["small"] = o + -(-width // 32) * 32
        assert used["small"] <= 12288, 0
        return place(name, shape, dt, "small", o)

    x_sb = place("x_sb", [TP, NT, D], F32, "x")
    tq_gu = place("tq_gu", [P, 2 * NF, D], BF16, "tq_gu")
    tq_d = place("tq_d", [P, KD, F], BF16, "tq_d")
    xnT = place("xnT", [P, NT, D], F32, "xz")
    z = place("z", [TP, NT, D], F32, "xz")
    raw = place("raw", [P, RAWS, RW], F32, "raw")
    w_sb = place("w_sb", [P, KD, 2 * D], F32, "w")
    hot_dst = place("hot_dst", [P, HOT, NT * WIN], BF16, "hot")
    SB, SBS = 8, 3
    hot_src = place("hot_src", [P, SBS, SB, P], BF16, "tq_d")
    deg_row = place("deg_row", [2, N], F32, "w")
    y_hi = place("y_hi", [TP, NT, D], F32R, "y")
    y_lo = place("y_lo", [TP, NT, D], F32R, "y", NT * D * 4)
    a_t = place("a_t", [TP, NT, N], F32R, "a")
    e_i = place("e_i", [P, 4, P], I32, "a")
    e_f = place("e_f", [P, 4, P], F32, "a", 4 * P * 4)
    x1nT = place("x1nT", [P, KD, N], F32, "w")
    x1_hi = place("x1_hi", [P, KD, N], F32R, "y")
    x1_lo = place("x1_lo", [P, KD, N], F32R, "y", KD * N * 4)
    t_gu = place("t_gu", [P, 2, 2, D], F32R, "a")
    t_d = place("t_d", [P, 2, D], F32R, "a", 16 * D)
    acc = place("acc", [P, KD, N], F32, "a", 24 * D)
    b4 = CW * 4
    HS = 4
    h_hi = place("h_hi", [P, HS, CW], F32R, "xz", 0)
    h_lo = place("h_lo", [P, HS, CW], F32R, "xz", HS * b4)
    g_acc = place("g_acc", [P, 2, CW], F32, "xz", 2 * HS * b4)
    u_acc = place("u_acc", [P, 2, CW], F32, "xz", (2 * HS + 2) * b4)
    sg = place("sg", [P, 2, CW], F32, "xz", (2 * HS + 4) * b4)
    hh = place("hh", [P, 2, CW], F32, "xz", (2 * HS + 6) * b4)
    d_one = place("d_one", [P, 3, 2, CW], F32, "a", 32512)
    assert (2 * HS + 8) * b4 <= at["w"] - at["xz"] and 24 * D + KD * N * 4 <= 32512 and 32512 + 6 * b4 <= NT * N * 4
    assert KD * N * 4 <= at["y"] - at["w"]
    o_sb = place("o_sb", [TP, NT, D], F32, "y")

    ident = small("ident", [P, P], F32)
    ident_b = small("ident_b", [P, P], BF16)
    ones = small("ones", [P, P], F32)
    ones_r = small("ones_r", [P, 2], F32R)
    eps = small("eps", [P, 1], F32)
    iota = small("iota", [P, 512], U16)
    win0 = small("win0", [P, NCP], F32)
    dst_f = small("dst_f", [P, NCP], F32)
    src_hi = small("src_hi", [P, NCP], F32)
    src_lo = small("src_lo", [P, NCP], F32)
    key = small("key", [P, NCP], F32)
    tmp = small("tmp", [P, NCP], F32)
    inside = small("inside", [P, 1], F32)
    flag = small("flag", [P, 1], I32)
    good = small("good", [P, 1], F32)
    bias_b = small("bias_b", [P, D], F32)
    absum = small("absum", [P, 132], F32)
    nscale = small("nscale", [P, 132], F32)
    th_hi = small("th_hi", [P, 132], F32)
    th_lo = small("th_lo", [P, 132], F32)
    bn = small("bn", [P, NT, 6], F32)
    mv = small("mv", [P, NT, 2], F32)
    sd = small("sd", [P, NT], F32)
    rs = small("rs", [P, NT], F32)
    rdeg = small("rdeg", [P, NT], F32)
    ss = small("ss", [P, NT], F32)
    nrm = small("nrm", [P, NT], F32)
    inv = small("inv", [P, NT], F32)
    mv1 = small("mv1", [P, NT, 2], F32)
    sd1 = small("sd1", [P, NT], F32)
    rs1 = small("rs1", [P, NT], F32)
    hot_gen = place("hot_gen", [P, NT * 50], BF16, "hot")
    src_gen = place("src_gen", [P, P], BF16, "hot", 1024)
    deg_sum = small("deg_sum", [P, NT], F32)
    blk0 = small("blk0", [P, 25], F32)
    xn = place("xn", [TP, 2, D], F32, "xn")

    with ExitStack() as ctx:
        bank = [ctx.enter_context(nc.psum_tensor(f"bank{i}", [P, 512], F32)) for i in range(8)]

        def bf(i):
            return bank[i][:, :].bitcast(BF16)

        def sem(name):
            return ctx.enter_context(nc.semaphore(name))

        const_done = sem("const_done")
        edges_in = sem("edges_in")
        x_in = [sem(f"x_in{t}") for t in range(NT)]
        w_in = sem("w_in")
        raw_in = [sem(f"raw_in{i}") for i in range(RAWS)]
        out_done = sem("out_done")
        prep = sem("prep")
        edges_T = sem("edges_T")
        bn_done = sem("bn_done")
        stats = sem("stats")
        root = sem("root")
        rstd = sem("rstd")
        normed = sem("normed")
        xn_T = sem("xn_T")
        xnT_done = sem("xnT_done")
        y_ready = sem("y_ready")
        z_ready = sem("z_ready")
        yhi_done = sem("yhi_done")
        ylo_done = sem("ylo_done")
        z_out = sem("z_out")
        z_done = sem("z_done")
        src_wide = sem("src_wide")
        hot_made = sem("hot_made")
        hot_used = sem("hot_used")
        block_done = sem("block_done")
        block_out = sem("block_out")
        abs_done = sem("abs_done")
        scales = sem("scales")
        above = sem("above")
        ternary = sem("ternary")

        SLOTS = 8 * NT
        FIRST = 6

        def chunks_in(slot):
            def upto(s):
                return 0 if s < FIRST else min(NC, -(-NC * (s - FIRST + 1) // (SLOTS - FIRST)))
            return range(upto(slot - 1), upto(slot))

        def window(c):
            k, off = divmod(STEP * c - LEAD, WIN)
            parts = [(k, off, 0, WIN - off), (k + 1, 0, WIN - off, off)]
            return [p for p in parts if 0 <= p[0] < NB and p[3]]

        first_chunk = [min(c for c in range(NC) if any(p[0] == k for p in window(c))) for k in range(NB)]
        last_chunk = [max(c for c in range(NC) if any(p[0] == k for p in window(c))) for k in range(NB)]

        def blocks_ending(slot):
            return [k for k in range(NB) if last_chunk[k] in chunks_in(slot)]

        loads = []
        for w in (w_gate, w_up):
            for f in range(NF):
                loads.append((w[f * P:(f + 1) * P, :], KD))
        for o in range(KD):
            for f in range(0, NF, 4):
                n = min(4, NF - f)
                loads.append((w_down[o * P:(o + 1) * P, f * P:(f + n) * P], n))
        job_load = [(l, i) for l, (_, n) in enumerate(loads) for i in range(n)]
        JOBS = len(job_load)
        load_end = [sum(n for _, n in loads[:l + 1]) for l in range(len(loads))]
        assert JOBS == 3 * NF * KD

        def tq_of(j):
            if j < 2 * NF * KD:
                return tq_gu[:, j // KD, (j % KD) * P:(j % KD + 1) * P]
            o, f = divmod(j - 2 * NF * KD, NF)
            return tq_d[:, o, f * P:(f + 1) * P]

        def raw_of(j):
            l, i = job_load[j]
            return raw[:, l % RAWS, i * P:(i + 1) * P]

        GU_JOBS, GU_LOADS = 2 * NF * KD, 2 * NF

        def jobs_in(slot, lag):
            def upto(s):
                return max(0, min(GU_JOBS, -(-GU_JOBS * (s - lag + 1) // (SLOTS - 6))))
            return range(upto(slot - 1), upto(slot))

        LN_GROUPS = [(0, 1), (1, 4), (4, NT)]

        GB, GC = 50, 32
        GK, GQ = N // GB, NCP // GC
        gen_hot = sem("gen_hot")
        gen_used = sem("gen_used")
        gen_block = sem("gen_block")
        gen_out = sem("gen_out")
        gen_sum = sem("gen_sum")
        gen_taken = sem("gen_taken")

        deg_rows = sem("deg_rows")
        deg_row_out = sem("deg_row_out")
        deg_ready = sem("deg_ready")
        rdeg_done = sem("rdeg_done")
        n_ready = sem("n_ready")
        hsum = sem("hsum")
        leaky = sem("leaky")
        squares = sem("squares")
        norms = sem("norms")
        inv_done = sem("inv_done")
        x1_done = sem("x1_done")
        stats1 = sem("stats1")
        root1 = sem("root1")
        rstd1 = sem("rstd1")
        normed1 = sem("normed1")
        x1n_T = sem("x1n_T")
        x1nT_done = sem("x1nT_done")
        hi_done = sem("hi_done")
        lo_done = sem("lo_done")

        UNITS = [(f, c) for f in range(NF) for c in range(len(CH))]
        NU = len(UNITS)
        LAG = 3
        TURN = ["G0", "U0", "D1", "G1", "U1", "D2", "G2", "U2", "D3", "G3", "U3", "D0"]
        BY_ACT = {"G0", "U0", "D1", "D2", "D3"}
        pieces = []
        for n in range(NU + LAG):
            for what in TURN:
                u = n - LAG if what[0] == "D" else n
                if 0 <= u < NU:
                    pieces.append((u, what))
        index = {p: i for i, p in enumerate(pieces)}
        RING = 7
        took = {}
        for i, (u, what) in enumerate(pieces):
            took[u, what] = 1 + sum((q[1] in BY_ACT) == (what in BY_ACT) for q in pieces[:i])
        piece_ready = sem("piece_ready")
        act_took = sem("act_took")
        dve_took = sem("dve_took")
        silu_done = sem("silu_done")
        h_done = sem("h_done")
        hhi_done = sem("hhi_done")
        hlo_done = sem("hlo_done")
        d_added = sem("d_added")
        t_ready = sem("t_ready")
        t_done = sem("t_done")
        o_T = sem("o_T")
        o_done = sem("o_done")

        def adds_to(u, o):
            return 3 * (u - 3) + o

        def took_sem(what):
            return act_took if what in BY_ACT else dve_took

        def bank_of(u, what):
            return bank[index[u, what] % RING]

        def general_dve(dve):
            any_outside = dve.value_load(flag[0:1, 0:1])
            with dve.If(any_outside):
                dve.wait_ge(block_out, NB)
                dve.wait_ge(hot_used, NC - 1)
                dve.sem_inc(gen_out, 1)
                dve.sem_inc(gen_taken, 1)
                for sweep in range(2):
                    with dve.Fori(0, GQ) as q:
                        with dve.Fori(0, GK) as k:
                            cs = bass.ds(q * GC, GC)
                            dve.drain()
                            dve.wait_ge(gen_sum, 1 + (sweep * GQ + q) * NT)
                            nc.vector.tensor_scalar(tmp[:, 0:GC], dst_f[:, cs], blk0[:, bass.ds(k, 1)], None, ALU.subtract)
                            dve.drain()
                            nc.vector.tensor_scalar(win0[:, 0:GC], tmp[:, 0:GC], 0.0, None, ALU.is_ge)
                            dve.drain()
                            nc.vector.scalar_tensor_tensor(out=win0[:, 0:GC], in0=tmp[:, 0:GC], scalar=float(GB - 1),
                                                           in1=win0[:, 0:GC], op0=ALU.is_le, op1=ALU.mult)
                            nc.vector.scalar_tensor_tensor(out=key[:, 0:GC], in0=src_hi[:, cs], scalar=float(GB),
                                                           in1=tmp[:, 0:GC], op0=ALU.mult, op1=ALU.add)
                            dve.drain()
                            nc.vector.scalar_tensor_tensor(out=tmp[:, 0:GC], in0=key[:, 0:GC], scalar=1.0, in1=win0[:, 0:GC],
                                                           op0=ALU.add, op1=ALU.mult)
                            dve.drain()
                            nc.vector.tensor_scalar(key[:, 0:GC], tmp[:, 0:GC], 1.0, None, ALU.subtract)
                            dve.drain()
                            nc.vector.tensor_copy(tmp[:, 0:GC], src_lo[:, cs])
                            dve.drain()
                            done = ((sweep * GQ + q) * GK + k) * GC
                            for j in range(GC):
                                dve.wait_ge(gen_used, 1 + done + j)
                                nc.vector.tensor_scalar(src_gen[:, 0:TP], iota[:, 0:TP], tmp[:, j:j + 1], None, ALU.is_equal)
                                nc.vector.tensor_scalar(hot_gen[:, 0:NT * GB], iota[:, 0:NT * GB], key[:, j:j + 1], None,
                                                        ALU.is_equal).then_inc(gen_hot, 1)
                            dve.wait_ge(gen_used, 1 + done + GC)
                            for s in range(NT):
                                last = nc.vector.tensor_scalar(a_t[:, s, bass.ds(k * GB, GB)], bank[7][0:TP, s * GB:(s + 1) * GB],
                                                               1.0, None, ALU.mult)
                            last.then_inc(gen_out, 1)
                        for t in range(NT):
                            dve.wait_ge(gen_sum, 1 + (sweep * GQ + q) * NT + t + 1)
                            if sweep == 0:
                                nc.vector.tensor_copy(tmp[0:TP, 0:1], bank[6][0:TP, 0:1])
                                dve.drain()
                                nc.vector.tensor_tensor(deg_sum[0:TP, t:t + 1], deg_sum[0:TP, t:t + 1], tmp[0:TP, 0:1],
                                                        ALU.add).then_inc(gen_taken, 1)
                            else:
                                nc.vector.scalar_tensor_tensor(out=z[:, t, :], in0=bank[6][0:TP, :], scalar=deg_sum[0:TP, t:t + 1],
                                                               in1=z[:, t, :], op0=ALU.mult, op1=ALU.add).then_inc(gen_taken, 1)
                    if sweep == 0:
                        dve.drain()
                        nc.vector.tensor_scalar(rdeg[0:TP, :], deg_sum[0:TP, :], 1.0, None, ALU.max)
                        dve.drain()
                        nc.vector.reciprocal(deg_sum[0:TP, :], rdeg[0:TP, :])
                        dve.drain()

        def general_pe(pe):
            any_outside = pe.value_load(flag[0:1, 0:1])
            with pe.If(any_outside):
                pe.wait_ge(z_done, NT)
                pe.wait_ge(ylo_done, NT)
                pe.sem_inc(gen_used, 1)
                pe.sem_inc(gen_sum, 1)
                for sweep in range(2):
                    with pe.Fori(0, GQ) as q:
                        with pe.Fori(0, GK) as k:
                            done = ((sweep * GQ + q) * GK + k) * GC
                            pe.wait_ge(gen_out, 1 + (sweep * GQ + q) * GK + k)
                            for j in range(GC):
                                pe.wait_ge(gen_hot, done + j + 1)
                                nc.tensor.matmul(bank[7][0:TP, 0:NT * GB], src_gen[:, 0:TP], hot_gen[:, 0:NT * GB],
                                                 start=j == 0, stop=j == GC - 1).then_inc(gen_used, 1)
                        pe.wait_ge(gen_out, 1 + (sweep * GQ + q + 1) * GK)
                        for t in range(NT):
                            pe.wait_ge(gen_taken, 1 + (sweep * GQ + q) * NT + t)
                            if sweep == 0:
                                for s in range(NT):
                                    last = nc.tensor.matmul(bank[6][0:TP, 0:2], a_t[:, s, t * TP:(t + 1) * TP], ones_r[0:TP, :],
                                                            start=s == 0, stop=s == NT - 1)
                            else:
                                for s in range(NT):
                                    for y in (y_hi, y_lo):
                                        last = nc.tensor.matmul(bank[6][0:TP, :], a_t[:, s, t * TP:(t + 1) * TP], y[:, s, :],
                                                                start=s == 0 and y is y_hi, stop=s == NT - 1 and y is y_lo)
                            last.then_inc(gen_sum, 1)

        block = ctx.enter_context(nc.Block())

        @block.sync
        def _(sp):
            sp.wait_ge(const_done, 1)
            for i, v in enumerate((src, dst)):
                sp.dma_start(e_i[:, 2 * i, :], v[0:P * P].rearrange("(c e) -> c e", e=P)).then_inc(edges_in, 16)
                n = E // P - P
                sp.dma_start(e_i[0:n, 2 * i + 1, :], v[P * P:(P + n) * P].rearrange("(c e) -> c e", e=P)).then_inc(edges_in, 16)
                sp.dma_start(e_i[n:n + 1, 2 * i + 1, 0:E - (P + n) * P],
                             v[(P + n) * P:E].rearrange("(c e) -> c e", c=1)).then_inc(edges_in, 16)
            for t in range(NT):
                sp.dma_start(x_sb[0:112, t, :], x[t * TP:t * TP + 112, :]).then_inc(x_in[t], 16)
                sp.dma_start(x_sb[112:TP, t, :], x[t * TP + 112:(t + 1) * TP, :]).then_inc(x_in[t], 16)
                if t == 0:
                    sp.dma_start(w_sb[:, :, 0:D], w_neigh.rearrange("(k p) n -> p k n", p=P)).then_inc(w_in, 16)
                    sp.dma_start(w_sb[:, :, D:2 * D], w_self.rearrange("(k p) n -> p k n", p=P)).then_inc(w_in, 16)
                    sp.dma_start(bias_b[:, :], bias.rearrange("(a n) -> a n", a=1).to_broadcast([P, D])).then_inc(w_in, 16)
            for l, (w, n) in enumerate(loads):
                if l >= RAWS:
                    sp.wait_ge(ternary, load_end[l - RAWS])
                sp.dma_start(raw[:, l % RAWS, 0:n * P], w).then_inc(raw_in[l % RAWS], 16)
            for t in range(NT):
                sp.wait_ge(o_done, t + 1)
                sp.dma_start(out[t * TP:t * TP + 112, :], o_sb[0:112, t, :]).then_inc(out_done, 16)
                sp.dma_start(out[t * TP + 112:(t + 1) * TP, :], o_sb[112:TP, t, :]).then_inc(out_done, 16)
            sp.wait_ge(out_done, 32 * NT)

        @block.gpsimd
        def _(pool):
            nc.gpsimd.memset(e_i[:], -1).then_inc(const_done, 1)
            nc.gpsimd.memset(ident[:], 1.0).then_inc(const_done, 1)
            nc.gpsimd.memset(ident_b[:], 1.0).then_inc(const_done, 1)
            pool.wait_ge(const_done, 3)
            for m in (ident, ident_b):
                nc.gpsimd.affine_select(out=m[:], in_=m[:], compare_op=ALU.is_equal, fill=0.0, base=0,
                                        pattern=[[-1, P]], channel_multiplier=1).then_inc(const_done, 1)
            nc.gpsimd.iota(win0[:], pattern=[[STEP, NCP]], base=-LEAD, channel_multiplier=0,
                           allow_small_or_imprecise_dtypes=True).then_inc(const_done, 1)
            nc.gpsimd.iota(iota[:], pattern=[[1, 512]], base=0, channel_multiplier=0,
                           allow_small_or_imprecise_dtypes=True).then_inc(const_done, 1)
            nc.gpsimd.iota(blk0[:], pattern=[[GB, GK]], base=0, channel_multiplier=0,
                           allow_small_or_imprecise_dtypes=True).then_inc(const_done, 1)
            nc.gpsimd.memset(ones[:], 1.0).then_inc(const_done, 1)
            nc.gpsimd.memset(eps[:], LN_EPS).then_inc(const_done, 1)
            nc.gpsimd.memset(deg_sum[:], 0.0).then_inc(const_done, 1)
            step = [0]

            def above_of(l):
                js = slice(load_end[l] - loads[l][1], load_end[l])
                pool.wait_ge(abs_done, load_end[l])
                nc.gpsimd.tensor_scalar(nscale[:, js], absum[:, js], -1.0 / P, -Q_EPS, ALU.mult, ALU.add).then_inc(scales, 1)
                pool.wait_ge(scales, step[0] + 1)
                nc.gpsimd.tensor_scalar(th_hi[:, js], nscale[:, js], -0.5, 0.0, ALU.mult, ALU.add).then_inc(scales, 1)
                nc.gpsimd.tensor_scalar(th_lo[:, js], nscale[:, js], 0.5, 0.0, ALU.mult, ALU.add).then_inc(scales, 1)
                step[0] += 3
                pool.wait_ge(scales, step[0])
                for j in range(js.start, js.stop):
                    nc.gpsimd.tensor_scalar(tq_of(j), raw_of(j), th_hi[:, j:j + 1], None, ALU.is_gt).then_inc(above, 1)

            for slot in range(SLOTS + 8):
                t, i = divmod(slot, 8)
                for j in jobs_in(slot, 1):
                    l, g = job_load[j]
                    if g == loads[l][1] - 1:
                        above_of(l)
                if i == 4 and 1 <= t <= NT:
                    if t == 1:
                        pool.wait_ge(w_in, 48)
                    pool.wait_ge(z_out, t)
                    nc.gpsimd.tensor_tensor(z[:, t - 1, :], z[:, t - 1, :], bias_b[0:TP, :], ALU.add).then_inc(z_done, 1)
            for l in range(GU_LOADS, len(loads)):
                above_of(l)

            for n in range(NU + LAG):
                if 1 <= n <= NU:
                    u = n - 1
                    w = CH[UNITS[u][1]][1]
                    pool.wait_ge(silu_done, u + 1)
                    pool.wait_ge(dve_took, took[u, "U3"])
                    if u >= 2:
                        pool.wait_ge(hlo_done, u - 1)
                    nc.gpsimd.tensor_tensor(hh[:, u % 2, 0:w], sg[:, u % 2, 0:w], u_acc[:, u % 2, 0:w], ALU.mult).then_inc(h_done, 1)
                if n >= LAG + 3:
                    u = n - LAG
                    s0, w = CH[UNITS[u][1]]
                    for o in range(1, KD):
                        pool.wait_ge(act_took, took[u, f"D{o}"])
                        if u >= 6:
                            pool.wait_ge(d_added, adds_to(u - 3, o))
                        to = acc[:, o, s0:s0 + w]
                        nc.gpsimd.tensor_tensor(to, to, d_one[:, o - 1, u % 2, 0:w], ALU.add).then_inc(d_added, 1)

        @block.scalar
        def _(act):
            def layernorm_root(g, ready, var, sdev, done):
                a, b = g
                act.wait_ge(ready, b)
                nc.scalar.activation(sdev[0:TP, a:b], var[0:TP, a:b, 1], ACT.Sqrt, bias=eps[0:TP, :]).then_inc(done, 1)

            def spread_src(b):
                if b >= SBS:
                    act.wait_ge(hot_used, SB * (b - SBS + 1))
                n = min(SB, NC - SB * b)
                nc.scalar.activation(hot_src[:, b % SBS, 0:n, 0:TP],
                                     src_lo[:, SB * b:SB * b + n, None].to_broadcast([P, n, TP]), ACT.Copy).then_inc(src_wide, 1)

            def batches_in(slot):
                cs = chunks_in(slot + 3)
                return [c // SB for c in cs if c % SB == 0]

            def abs_of(j):
                l, _ = job_load[j]
                act.wait_ge(raw_in[l % RAWS], 16 * (l // RAWS + 1))
                nc.scalar.activation(tq_of(j), raw_of(j), ACT.Abs, accum_out=absum[:, j:j + 1]).then_inc(abs_done, 1)

            act.wait_ge(const_done, 11)
            for slot in range(SLOTS + 8):
                t, i = divmod(slot, 8)
                if slot == 3:
                    act.wait_ge(prep, 5)
                for b in batches_in(slot):
                    spread_src(b)
                if slot == 0:
                    layernorm_root(LN_GROUPS[0], stats, mv, sd, root)
                    act.wait_ge(xn_T, 1)
                    nc.scalar.activation(xnT[:, 0, 0:KD * TP], bank[3][:, 0:KD * TP], ACT.Copy).then_inc(xnT_done, 1)
                    layernorm_root(LN_GROUPS[1], stats, mv, sd, root)
                if slot == 4:
                    layernorm_root(LN_GROUPS[2], stats, mv, sd, root)
                if i == 1 and 1 <= t <= NT:
                    act.wait_ge(y_ready, t)
                    nc.scalar.activation(y_hi[:, t - 1, :], bank[4 + (t - 1) % 2][0:TP, :], ACT.Copy).then_inc(yhi_done, 1)
                if i == 2 and 1 <= t <= NT:
                    act.wait_ge(z_ready, t)
                    nc.scalar.activation(z[:, t - 1, :], bank[6 + (t - 1) % 2][0:TP, :], ACT.Copy).then_inc(z_out, 1)
                if i == 5 and t + 1 < NT:
                    act.wait_ge(xn_T, t + 2)
                    nc.scalar.activation(xnT[:, t + 1, 0:KD * TP], bank[3][:, 0:KD * TP], ACT.Copy).then_inc(xnT_done, 1)
                if slot < SLOTS:
                    for j in jobs_in(slot, 0):
                        abs_of(j)
                    for k in blocks_ending(slot):
                        act.wait_ge(block_done, k + 1)
                        n = min(WIN, N - k * WIN)
                        nc.scalar.activation(
                            a_t[:, :, k * WIN:k * WIN + n],
                            bank[k % 3][0:TP, 0:NT * WIN].rearrange("p (s d) -> p s d", d=WIN)[:, :, 0:n],
                            ACT.Copy).then_inc(block_out, 1)
            for c, (s0, n) in enumerate(CH):
                act.wait_ge(deg_rows, c + 1)
                nc.scalar.activation(deg_row[:, s0:s0 + n], bank[1 + c][0:2, 0:n], ACT.Copy).then_inc(deg_row_out, 1)
            for n in range(NT + 4):
                if n < len(loads) - GU_LOADS:
                    l = GU_LOADS + n
                    for j in range(load_end[l] - loads[l][1], load_end[l]):
                        abs_of(j)
                if n < NT:
                    act.wait_ge(leaky, n + 1)
                    if n >= 1:
                        act.wait_ge(squares, n)
                    nc.scalar.activation(bank[3][0:TP, :], z[:, n, :], ACT.Square, accum_out=ss[0:TP, n:n + 1]).then_inc(squares, 1)
                    act.wait_ge(squares, n + 1)
                    nc.scalar.activation(nrm[0:TP, n:n + 1], ss[0:TP, n:n + 1], ACT.Sqrt).then_inc(norms, 1)
                if 1 <= n <= NT:
                    act.wait_ge(stats1, n)
                    nc.scalar.activation(sd1[0:TP, n - 1:n], mv1[0:TP, n - 1:n, 1], ACT.Sqrt, bias=eps[0:TP, :]).then_inc(root1, 1)
                if 3 <= n < NT + 3:
                    t = n - 3
                    act.wait_ge(x1n_T, t + 1)
                    nc.scalar.activation(x1nT[:, :, t * TP:(t + 1) * TP],
                                         bank[4 + t % 2][:, 0:KD * TP].rearrange("p (k s) -> p k s", k=KD),
                                         ACT.Copy).then_inc(x1nT_done, 1)

            def ternary_out(f, down):
                act.wait_ge(t_ready, 2 * f + 1 + down)
                if not down:
                    if f >= 2:
                        act.wait_ge(piece_ready, index[3 * (f - 2) + 2, "U3"] + 1)
                    nc.scalar.activation(t_gu[:, f % 2, :, :].rearrange("p a d -> p (a d)"), bf(7)[:, 0:2 * D],
                                         ACT.Copy).then_inc(t_done, 1)
                else:
                    if f >= 2:
                        act.wait_ge(piece_ready, index[3 * (f - 2) + 2, "D0"] + 1)
                    nc.scalar.activation(t_d[:, f % 2, :], bf(7)[:, 0:D], ACT.Copy).then_inc(t_done, 1)

            act.wait_ge(n_ready, NT)
            ternary_out(0, 0)
            for c, (s0, n) in enumerate(CH):
                act.wait_ge(x1nT_done, NT)
                nc.scalar.activation(x1_hi[:, :, s0:s0 + n], x1nT[:, :, s0:s0 + n], ACT.Copy).then_inc(hi_done, 1)
            ternary_out(0, 1)

            def take(u, what, to):
                f, c = UNITS[u]
                n = CH[c][1]
                k = int(what[1])
                j = {"G": 4 * f + k, "U": 4 * NF + 4 * f + k, "D": 8 * NF + NF * k + f}[what[0]]
                act.wait_ge(piece_ready, index[u, what] + 1)
                nc.scalar.activation(to, bank_of(u, what)[:, 0:n], ACT.Copy, scale=nscale[:, j:j + 1]).then_inc(act_took, 1)

            for n in range(NU + LAG):
                f, c = UNITS[n] if n < NU else (NF, 0)
                if n < NU:
                    w = CH[c][1]
                    if n >= 2:
                        act.wait_ge(silu_done, n - 1)
                    take(n, "G0", g_acc[:, n % 2, 0:w])
                    if n >= 2:
                        act.wait_ge(h_done, n - 1)
                    take(n, "U0", u_acc[:, n % 2, 0:w])
                if 1 <= n <= NU:
                    u = n - 1
                    wu = CH[UNITS[u][1]][1]
                    act.wait_ge(dve_took, took[u, "G3"])
                    nc.scalar.activation(sg[:, u % 2, 0:wu], g_acc[:, u % 2, 0:wu], ACT.Silu).then_inc(silu_done, 1)
                for what in ("D1", "D2", "D3"):
                    if n >= LAG:
                        v = n - LAG
                        fv, cv = UNITS[v]
                        s0, wv = CH[cv]
                        o = int(what[1])
                        if fv == 0:
                            take(v, what, acc[:, o, s0:s0 + wv])
                        else:
                            if v >= 5:
                                act.wait_ge(d_added, adds_to(v - 2, o))
                            take(v, what, d_one[:, o - 1, v % 2, 0:wv])
                    if what == "D2" and 1 <= n <= NU:
                        act.wait_ge(h_done, u + 1)
                        if u >= HS:
                            act.wait_ge(piece_ready, index[u - HS, "D0"] + 1)
                        nc.scalar.activation(h_hi[:, u % HS, 0:wu], hh[:, u % 2, 0:wu], ACT.Copy).then_inc(hhi_done, 1)
                if n < NU and f + 1 < NF:
                    if c == 0:
                        ternary_out(f + 1, 0)
                    if c == 2:
                        ternary_out(f + 1, 1)

        @block.vector
        def _(dve):
            steps = [0]

            def link(ins):
                steps[0] += 1
                ins.then_inc(prep, 1)
                dve.wait_ge(prep, steps[0])

            def normalize(t):
                if t >= 2:
                    dve.wait_ge(xn_T, t - 1)
                nc.vector.tensor_scalar(xn[:, t % 2, :], x_sb[:, t, :], mv[0:TP, t, 0:1], rs[0:TP, t:t + 1],
                                        ALU.subtract, ALU.mult).then_inc(normed, 1)

            def statistics(g):
                for t in range(*g):
                    dve.wait_ge(x_in[t], 32)
                    nc.vector.bn_stats(bn[0:TP, t, :], x_sb[:, t, :]).then_inc(bn_done, 1)
                for t in range(*g):
                    dve.wait_ge(bn_done, t + 1)
                    nc.vector.bn_aggr(mv[0:TP, t, :], bn[0:TP, t, :]).then_inc(stats, 1)

            def reciprocals(i):
                a, b = LN_GROUPS[i]
                dve.wait_ge(root, i + 1)
                nc.vector.reciprocal(rs[0:TP, a:b], sd[0:TP, a:b]).then_inc(rstd, 1)
                dve.wait_ge(rstd, i + 1)

            def ternary_of(j):
                dve.wait_ge(above, j + 1)
                nc.vector.scalar_tensor_tensor(out=tq_of(j), in0=raw_of(j), scalar=th_lo[:, j:j + 1], in1=tq_of(j),
                                               op0=ALU.is_lt, op1=ALU.subtract).then_inc(ternary, 1)

            dve.wait_ge(const_done, 11)
            nc.vector.tensor_copy(ones_r[:], ones[:, 0:2]).then_inc(prep, 1)
            steps[0] += 1
            dve.wait_ge(edges_in, 96)
            link(nc.vector.tensor_copy(e_f[:], e_i[:]))
            statistics(LN_GROUPS[0])
            reciprocals(0)
            normalize(0)
            dve.wait_ge(edges_T, 1)
            srcs, dsts = bank[5][:, 0:NCP], bank[5][:, NCP:2 * NCP]
            nc.vector.tensor_copy(dst_f[:], dsts).then_inc(prep, 1)
            steps[0] += 1
            link(nc.vector.tensor_scalar(tmp[:], srcs, (TP - 1) / 2, 1.0 / TP, ALU.subtract, ALU.mult))
            link(nc.vector.tensor_scalar(src_hi[:], tmp[:], ROUND, ROUND, ALU.add, ALU.subtract))
            link(nc.vector.scalar_tensor_tensor(out=src_lo[:], in0=src_hi[:], scalar=-float(TP), in1=srcs, op0=ALU.mult, op1=ALU.add))
            link(nc.vector.tensor_tensor(tmp[:], dst_f[:], win0[:], ALU.subtract))
            link(nc.vector.tensor_scalar(key[:], tmp[:], 0.0, None, ALU.is_ge))
            link(nc.vector.scalar_tensor_tensor(out=win0[:], in0=tmp[:], scalar=float(WIN - 1), in1=key[:], op0=ALU.is_le,
                                                op1=ALU.mult, accum_out=inside[:]))
            link(nc.vector.scalar_tensor_tensor(out=key[:], in0=src_hi[:], scalar=float(WIN), in1=tmp[:], op0=ALU.mult, op1=ALU.add))
            link(nc.vector.scalar_tensor_tensor(out=tmp[:], in0=key[:], scalar=1.0, in1=win0[:], op0=ALU.add, op1=ALU.mult))
            link(nc.vector.tensor_scalar(key[:], tmp[:], 1.0, None, ALU.subtract))
            statistics(LN_GROUPS[1])
            reciprocals(1)
            normalize(1)
            dve.wait_ge(edges_T, 2)
            nc.vector.tensor_scalar(good[:], bank[6][:, 0:1], float(E), None, ALU.is_equal).then_inc(prep, 1)
            nc.vector.tensor_scalar(flag[:], bank[6][:, 0:1], float(E), None, ALU.is_lt).then_inc(prep, 1)
            steps[0] += 2

            for slot in range(SLOTS + 8):
                t, i = divmod(slot, 8)
                if slot == 3:
                    statistics(LN_GROUPS[2])
                if slot == 5:
                    reciprocals(2)
                if i == 0 and 1 <= t and t + 1 < NT:
                    normalize(t + 1)
                if i == 2 and 1 <= t <= NT:
                    dve.wait_ge(yhi_done, t)
                    nc.vector.tensor_tensor(y_lo[:, t - 1, :], bank[4 + (t - 1) % 2][0:TP, :],
                                            y_hi[:, t - 1, :].bitcast(F32), ALU.subtract).then_inc(ylo_done, 1)
                if slot < SLOTS:
                    for c in chunks_in(slot):
                        if c % SB == 0:
                            b, n = c // SB, min(SB, NC - c)
                            dve.wait_ge(src_wide, b + 1)
                            nc.vector.tensor_tensor(hot_src[:, b % SBS, 0:n, 0:TP], iota[:, None, 0:TP].to_broadcast([P, n, TP]),
                                                    hot_src[:, b % SBS, 0:n, 0:TP], ALU.is_equal)
                        if c >= HOT:
                            dve.wait_ge(hot_used, c - HOT + 1)
                        nc.vector.tensor_scalar(hot_dst[:, c % HOT, :], iota[:, 0:NT * WIN], key[:, c:c + 1], None,
                                                ALU.is_equal).then_inc(hot_made, 1)
                for j in jobs_in(slot, 4):
                    ternary_of(j)

            general_dve(dve)

            dve.wait_ge(deg_ready, 1)
            nc.vector.tensor_scalar(rdeg[0:TP, :], bank[2][0:TP, 0:NT], 1.0, None, ALU.max).then_inc(rdeg_done, 1)
            dve.wait_ge(rdeg_done, 1)
            nc.vector.reciprocal(rs[0:TP, :], rdeg[0:TP, :]).then_inc(rdeg_done, 1)
            dve.wait_ge(rdeg_done, 2)
            nc.vector.tensor_scalar(rdeg[0:TP, :], rs[0:TP, :], good[0:TP, :], None, ALU.mult).then_inc(rdeg_done, 1)
            dve.wait_ge(rdeg_done, 3)
            for n in range(NT + 2):
                if n < NT:
                    dve.wait_ge(n_ready, n + 1)
                    dve.wait_ge(z_done, n + 1)
                    nc.vector.scalar_tensor_tensor(out=z[:, n, :], in0=bank[n % 2][0:TP, :], scalar=rdeg[0:TP, n:n + 1],
                                                   in1=z[:, n, :], op0=ALU.mult, op1=ALU.add).then_inc(hsum, 1)
                if 1 <= n <= NT:
                    t = n - 1
                    dve.wait_ge(norms, t + 1)
                    nc.vector.tensor_scalar(nrm[0:TP, t:t + 1], nrm[0:TP, t:t + 1], NORM_EPS, None, ALU.max).then_inc(inv_done, 1)
                    dve.wait_ge(inv_done, 2 * t + 1)
                    nc.vector.reciprocal(inv[0:TP, t:t + 1], nrm[0:TP, t:t + 1]).then_inc(inv_done, 1)
                    if n < NT:
                        dve.wait_ge(hsum, n + 1)
                        nc.vector.scalar_tensor_tensor(out=z[:, n, :], in0=z[:, n, :], scalar=SLOPE, in1=z[:, n, :],
                                                       op0=ALU.mult, op1=ALU.max).then_inc(leaky, 1)
                    dve.wait_ge(inv_done, 2 * t + 2)
                    nc.vector.scalar_tensor_tensor(out=x_sb[:, t, :], in0=z[:, t, :], scalar=inv[0:TP, t:t + 1],
                                                   in1=x_sb[:, t, :], op0=ALU.mult, op1=ALU.add).then_inc(x1_done, 1)
                elif n < NT:
                    dve.wait_ge(hsum, n + 1)
                    nc.vector.scalar_tensor_tensor(out=z[:, n, :], in0=z[:, n, :], scalar=SLOPE, in1=z[:, n, :],
                                                   op0=ALU.mult, op1=ALU.max).then_inc(leaky, 1)
                if 2 <= n:
                    t = n - 2
                    dve.wait_ge(root1, t + 1)
                    nc.vector.reciprocal(rs1[0:TP, t:t + 1], sd1[0:TP, t:t + 1]).then_inc(rstd1, 1)
                if 1 <= n <= NT:
                    t = n - 1
                    dve.wait_ge(x1_done, t + 1)
                    nc.vector.bn_stats(bn[0:TP, t, :], x_sb[:, t, :]).then_inc(bn_done, 1)
                    dve.wait_ge(bn_done, NT + t + 1)
                    nc.vector.bn_aggr(mv1[0:TP, t, :], bn[0:TP, t, :]).then_inc(stats1, 1)
                if 2 <= n:
                    t = n - 2
                    dve.wait_ge(rstd1, t + 1)
                    if t >= 2:
                        dve.wait_ge(x1n_T, t - 1)
                    nc.vector.tensor_scalar(xn[:, t % 2, :], x_sb[:, t, :], mv1[0:TP, t, 0:1], rs1[0:TP, t:t + 1],
                                            ALU.subtract, ALU.mult).then_inc(normed1, 1)
                if 1 <= n:
                    l = GU_LOADS + n - 1
                    for j in range(load_end[l] - loads[l][1], load_end[l]):
                        ternary_of(j)
            for j in range(load_end[-2], JOBS):
                ternary_of(j)
            for c, (s0, n) in enumerate(CH):
                dve.wait_ge(hi_done, c + 1)
                nc.vector.tensor_tensor(x1_lo[:, :, s0:s0 + n], x1nT[:, :, s0:s0 + n], x1_hi[:, :, s0:s0 + n].bitcast(F32),
                                        ALU.subtract).then_inc(lo_done, 1)

            def take(u, what):
                f, c = UNITS[u]
                s0, n = CH[c]
                k = int(what[1])
                j = {"G": 4 * f + k, "U": 4 * NF + 4 * f + k, "D": 8 * NF + NF * k + f}[what[0]]
                to = {"G": g_acc[:, u % 2, 0:n], "U": u_acc[:, u % 2, 0:n], "D": acc[:, k, s0:s0 + n]}[what[0]]
                dve.wait_ge(piece_ready, index[u, what] + 1)
                if what == "G1":
                    dve.wait_ge(act_took, took[u, "G0"])
                elif what == "U1":
                    dve.wait_ge(act_took, took[u, "U0"])
                elif what[0] != "D":
                    dve.wait_ge(dve_took, took[u, what[0] + str(k - 1)])
                elif f:
                    dve.wait_ge(dve_took, took[u - 3, what])
                if what[0] == "D" and f == 0:
                    nc.vector.tensor_scalar(to, bank_of(u, what)[:, 0:n], nscale[:, j:j + 1], None, ALU.mult).then_inc(dve_took, 1)
                else:
                    nc.vector.scalar_tensor_tensor(out=to, in0=bank_of(u, what)[:, 0:n], scalar=nscale[:, j:j + 1], in1=to,
                                                   op0=ALU.mult, op1=ALU.add).then_inc(dve_took, 1)

            for n in range(NU + LAG):
                for what in TURN:
                    u = n - LAG if what[0] == "D" else n
                    if 0 <= u < NU and what not in BY_ACT:
                        take(u, what)
                if 1 <= n <= NU:
                    u = n - 1
                    w = CH[UNITS[u][1]][1]
                    dve.wait_ge(hhi_done, u + 1)
                    nc.vector.tensor_tensor(h_lo[:, u % HS, 0:w], hh[:, u % 2, 0:w], h_hi[:, u % HS, 0:w].bitcast(F32),
                                            ALU.subtract).then_inc(hlo_done, 1)
            for t in range(NT):
                dve.wait_ge(o_T, t + 1)
                nc.vector.tensor_tensor(o_sb[:, t, :], bank[t % 4][0:TP, :], x_sb[:, t, :], ALU.add).then_inc(o_done, 1)

        @block.tensor
        def _(pe):
            def transpose_xn(t, ready, to, done):
                pe.wait_ge(ready, t + 1)
                for k in range(KD):
                    last = nc.tensor.transpose(to[:, k * TP:(k + 1) * TP], xn[:, t % 2, k * P:(k + 1) * P], ident[0:TP, 0:TP])
                last.then_inc(done, 1)

            def add_chunk(c):
                pe.wait_ge(hot_made, c + 1)
                parts = window(c)
                for k, d0, w0, n in parts:
                    if c == first_chunk[k] and k >= 3:
                        pe.wait_ge(block_out, k - 2)
                    last = nc.tensor.matmul(
                        bank[k % 3][0:TP, 0:NT * WIN].rearrange("p (s d) -> p s d", d=WIN)[:, :, d0:d0 + n],
                        hot_src[:, c // SB % SBS, c % SB, 0:TP],
                        hot_dst[:, c % HOT, :].rearrange("p (s d) -> p s d", d=WIN)[:, :, w0:w0 + n],
                        start=c == first_chunk[k], stop=c == last_chunk[k], skip_group_check=True)
                    if c == last_chunk[k]:
                        last.then_inc(block_done, 1)
                    elif (k, d0, w0, n) == parts[-1]:
                        last.then_inc(hot_used, 1)

            pe.wait_ge(const_done, 11)
            pe.wait_ge(prep, 2)
            for i, (rows, col) in enumerate(((P, 0), (32, P), (P, NCP), (32, NCP + P))):
                last = nc.tensor.transpose(bank[5][:, col:col + rows], e_f[0:rows, i, :], ident[0:rows, 0:rows])
            last.then_inc(edges_T, 1)
            transpose_xn(0, normed, bank[3], xn_T)
            for slot in range(SLOTS):
                t, i = divmod(slot, 8)
                if i == 0:
                    pe.wait_ge(xnT_done, t + 1)
                    if t == 0:
                        pe.wait_ge(w_in, 48)
                    if t >= 2:
                        pe.wait_ge(ylo_done, t - 1)
                if i == 4 and t >= 2:
                    pe.wait_ge(z_out, t - 1)
                if slot == 4:
                    pe.wait_ge(prep, 9)
                    nc.tensor.matmul(bank[6][:, 0:1], ones[:], inside[:], start=True, stop=True).then_inc(edges_T, 1)
                    pe.wait_ge(prep, 14)
                k, half = i % 4, i // 4
                to = bank[(6 if half else 4) + t % 2]
                last = nc.tensor.matmul(to[0:TP, :], xnT[:, t, k * TP:(k + 1) * TP], w_sb[:, k, half * D:(half + 1) * D],
                                        start=k == 0, stop=k == KD - 1)
                if k == KD - 1:
                    last.then_inc(z_ready if half else y_ready, 1)
                if i == 4 and t + 1 < NT:
                    transpose_xn(t + 1, normed, bank[3], xn_T)
                for c in chunks_in(slot):
                    add_chunk(c)

            general_pe(pe)

            pe.wait_ge(block_out, NB)
            pe.wait_ge(prep, 1)
            for c, (s0, n) in enumerate(CH):
                for s in range(NT):
                    last = nc.tensor.matmul(bank[1 + c][0:2, 0:n], ones_r[0:TP, :], a_t[:, s, s0:s0 + n],
                                            start=s == 0, stop=s == NT - 1)
                last.then_inc(deg_rows, 1)
            pe.wait_ge(ylo_done, NT)
            for n in range(NT + 3):
                if n < NT:
                    if n >= 2:
                        pe.wait_ge(hsum, n - 1)
                    if n == 1:
                        pe.wait_ge(deg_row_out, len(CH))
                        for t in range(NT):
                            last = nc.tensor.matmul(bank[2][0:TP, t:t + 1], deg_row[0:1, t * TP:(t + 1) * TP], ones[0:1, 0:1],
                                                    start=True, stop=True, skip_group_check=True)
                        last.then_inc(deg_ready, 1)
                    for s in range(NT):
                        for y in (y_hi, y_lo):
                            last = nc.tensor.matmul(bank[n % 2][0:TP, :], a_t[:, s, n * TP:(n + 1) * TP], y[:, s, :],
                                                    start=s == 0 and y is y_hi, stop=s == NT - 1 and y is y_lo)
                    last.then_inc(n_ready, 1)
                if 3 <= n:
                    t = n - 3
                    if t >= 2:
                        pe.wait_ge(x1nT_done, t - 1)
                    transpose_xn(t, normed1, bank[4 + t % 2], x1n_T)

            def ternary_in(f, down):
                pe.wait_ge(ternary, JOBS if down else GU_JOBS)
                if 2 * f + down:
                    pe.wait_ge(t_done, 2 * f + down)
                if not down:
                    for a in range(2):
                        for k in range(KD):
                            last = nc.tensor.transpose(bf(7)[:, a * D + k * P:a * D + (k + 1) * P],
                                                       tq_gu[:, a * NF + f, k * P:(k + 1) * P], ident_b[:])
                else:
                    for o in range(KD):
                        last = nc.tensor.transpose(bf(7)[:, o * P:(o + 1) * P], tq_d[:, o, f * P:(f + 1) * P], ident_b[:])
                last.then_inc(t_ready, 1)

            ternary_in(0, 0)
            ternary_in(0, 1)
            pe.wait_ge(x1nT_done, NT)
            for i, (u, what) in enumerate(pieces):
                f, c = UNITS[u]
                s0, n = CH[c]
                k = int(what[1])
                if what == "G0":
                    if u < 3:
                        pe.wait_ge(lo_done, u + 1)
                    if c == 0:
                        pe.wait_ge(t_done, 2 * f + 1)
                if what == "D1":
                    pe.wait_ge(hlo_done, u + 1)
                    if c == 0:
                        pe.wait_ge(t_done, 2 * f + 2)
                if i >= RING:
                    old = pieces[i - RING]
                    pe.wait_ge(took_sem(old[1]), took[old])
                if what[0] == "D":
                    w = t_d[:, f % 2, k * P:(k + 1) * P]
                    parts = (h_hi[:, u % HS, 0:n], h_lo[:, u % HS, 0:n])
                else:
                    w = t_gu[:, f % 2, int(what[0] == "U"), k * P:(k + 1) * P]
                    parts = (x1_hi[:, k, s0:s0 + n], x1_lo[:, k, s0:s0 + n])
                for h in range(2):
                    last = nc.tensor.matmul(bank_of(u, what)[:, 0:n], w, parts[h], start=h == 0, stop=h == 1)
                last.then_inc(piece_ready, 1)
                if what == "U3" and f + 1 < NF:
                    if c == 0:
                        ternary_in(f + 1, 0)
                    if c == 2:
                        ternary_in(f + 1, 1)
            pe.wait_ge(dve_took, took[NU - 1, "D0"])
            pe.wait_ge(act_took, took[NU - 1, "D3"])
            for t in range(NT):
                for u in range(NU - 3, NU):
                    s0, n = CH[UNITS[u][1]]
                    if s0 < (t + 1) * TP and t * TP < s0 + n:
                        pe.wait_ge(d_added, adds_to(u, KD - 1))
                if t >= 4:
                    pe.wait_ge(o_done, t - 3)
                for k in range(KD):
                    last = nc.tensor.transpose(bank[t % 4][0:TP, k * P:(k + 1) * P], acc[:, k, t * TP:(t + 1) * TP], ident[:])
                last.then_inc(o_T, 1)


_INS = ["x", "src", "dst", "L0_gnn_W_self", "L0_gnn_W_neigh", "L0_gnn_b", "L0_ffn_w_gate", "L0_ffn_w_up", "L0_ffn_w_down"]


def kernel(**inputs):
    import numpy as np
    import concourse.bacc as bacc
    from concourse.bass_utils import run_bass_kernel_spmd

    nc = bacc.Bacc("TRN2", target_bir_lowering=False, num_devices=1)
    arrays, args = {}, []
    for name in _INS:
        a = np.ascontiguousarray(inputs[name])
        arrays[f"in_{name}"] = a
        args.append(nc.dram_tensor(f"in_{name}", a.shape, mybir.dt.from_np(a.dtype), kind="ExternalInput").ap())
    shape = arrays["in_x"].shape
    args.append(nc.dram_tensor("out_x", shape, F32, kind="ExternalOutput").ap())
    gnn_ffn(nc, *args)
    r = run_bass_kernel_spmd(nc, [arrays], core_ids=[0])
    return r.results[0]["out_x"]
```

```python
from contextlib import ExitStack

import concourse.bass as bass
from concourse import mybir

F32 = mybir.dt.float32
F32R = mybir.dt.float32r
BF16 = mybir.dt.bfloat16
U16 = mybir.dt.uint16
I32 = mybir.dt.int32
ALU = mybir.AluOpType
ACT = mybir.ActivationFunctionType

P = 128
WIN = 40
ROUND = 12582912.0
LN_EPS = 1e-5
NORM_EPS = 1e-12
Q_EPS = 1e-5
SLOPE = 0.01


def gnn_ffn(nc, x, src, dst, w_self, w_neigh, bias, w_gate, w_up, w_down, out):
    N, D = x.shape
    E = src.shape[0]
    F = w_gate.shape[0]
    TP = 125
    NT = N // TP
    KD = D // P
    NF = F // P
    NC = -(-E // P)
    NCP = 160
    EPD = E // N
    STEP = P // EPD
    LEAD = (WIN - STEP) // 2
    NB = -(-N // WIN)
    assert (N, D, E, F) == (TP * NT, 512, EPD * N, 1408) and NC == 157 and WIN % STEP == 0

    HOT = 5
    RW = 4 * P
    RAWS = 4
    ROW = [(0, 418), (418, 416), (834, 416)]
    ROW_BANK = [2, 3, 1]
    TQ = 126
    CT = [(0, 3), (3, 6), (6, NT)]
    CW = 512

    base = 17408
    at = {}
    for name, size in (
        ("x", NT * D * 4), ("tq_gu", 2 * NF * D * 2), ("tq_d", KD * F * 2), ("xz", NT * D * 4), ("raw", RAWS * RW * 4),
        ("w", KD * 2 * D * 4), ("hot", HOT * NT * WIN * 2), ("y", 2 * NT * D * 4), ("a", NT * N * 4),
        ("xn", 2 * D * 4), ("small", 12288),
    ):
        at[name] = base
        base += -(-size // 32) * 32
    assert base <= 229368, base
    used = {"small": 0}

    def place(name, shape, dt, region, offset=0):
        return nc.alloc_sbuf_tensor_at(name, shape, dt, offset=at[region] + offset)

    def small(name, shape, dt):
        width = {F32: 4, F32R: 4, I32: 4, BF16: 2, U16: 2}[dt]
        for n in shape[1:]:
            width *= n
        o = used["small"]
        used["small"] = o + -(-width // 32) * 32
        assert used["small"] <= 12288, 0
        return place(name, shape, dt, "small", o)

    x_sb = place("x_sb", [TP, NT, D], F32, "x")
    tq_gu = place("tq_gu", [P, 2 * NF, D], BF16, "tq_gu")
    tq_d = place("tq_d", [P, KD, F], BF16, "tq_d")
    xnT = place("xnT", [P, NT, D], F32, "xz")
    z = place("z", [TP, NT, D], F32, "xz")
    raw = place("raw", [P, RAWS, RW], F32, "raw")
    w_sb = place("w_sb", [P, KD, 2 * D], F32, "w")
    hot_dst = place("hot_dst", [P, HOT, NT * WIN], BF16, "hot")
    SB, SBS = 8, 3
    hot_src = place("hot_src", [P, SBS, SB, P], BF16, "tq_d")
    deg_row = place("deg_row", [2, N], F32, "w")
    y_hi = place("y_hi", [TP, NT, D], F32R, "y")
    y_lo = place("y_lo", [TP, NT, D], F32R, "y", NT * D * 4)
    a_t = place("a_t", [TP, NT, N], F32R, "a")
    e_i = place("e_i", [P, 4, P], I32, "a")
    e_f = place("e_f", [P, 4, P], F32, "a", 4 * P * 4)
    x1_hi = place("x1_hi", [P, NT, KD, TQ], F32R, "w")
    x1_lo = place("x1_lo", [P, NT, KD * P], F32R, "xz")
    h_slots = 4
    h_hi = place("h_hi", [P, h_slots, CW], F32R, "y")
    h_lo = place("h_lo", [P, h_slots, CW], F32R, "y", h_slots * CW * 4)
    g_acc = place("g_acc", [P, 2, CW], F32, "y", 8 * CW * 4)
    u_acc = place("u_acc", [P, 2, CW], F32, "y", 10 * CW * 4)
    sg = place("sg", [P, 2, CW], F32, "y", 12 * CW * 4)
    hh = place("hh", [P, 2, CW], F32, "y", 14 * CW * 4)
    t_gu = place("t_gu", [P, 2, 2, D], F32R, "a")
    t_d = place("t_d", [P, 2, D], F32R, "a", 16 * D)
    acc = place("acc", [P, KD, NT * TQ], F32, "a", 24 * D)
    d_one = place("d_one", [P, 3, 2, CW], F32, "a", 32512)
    assert 24 * D + KD * NT * TQ * 4 <= 32512 and 32512 + 6 * CW * 4 <= NT * N * 4
    assert 16 * CW * 4 <= at["a"] - at["y"] and NT * KD * TQ * 4 <= at["y"] - at["w"]

    ident = small("ident", [P, P], F32)
    ident_b = small("ident_b", [P, P], BF16)
    ones = small("ones", [P, P], F32)
    ones_r = small("ones_r", [P, 2], F32R)
    eps = small("eps", [P, 1], F32)
    iota = small("iota", [P, 512], U16)
    win0 = small("win0", [P, NCP], F32)
    dst_f = small("dst_f", [P, NCP], F32)
    src_hi = small("src_hi", [P, NCP], F32)
    src_lo = small("src_lo", [P, NCP], F32)
    key = small("key", [P, NCP], F32)
    tmp = small("tmp", [P, NCP], F32)
    inside = small("inside", [P, 1], F32)
    flag = small("flag", [P, 1], I32)
    good = small("good", [P, 1], F32)
    bias_b = small("bias_b", [P, D], F32)
    absum = small("absum", [P, 132], F32)
    nscale = small("nscale", [P, 132], F32)
    th_hi = small("th_hi", [P, 132], F32)
    th_lo = small("th_lo", [P, 132], F32)
    bn = small("bn", [P, NT, 6], F32)
    mv = small("mv", [P, NT, 2], F32)
    sd = small("sd", [P, NT], F32)
    rs = small("rs", [P, NT], F32)
    rdeg = small("rdeg", [P, NT], F32)
    ss = small("ss", [P, NT], F32)
    nrm = small("nrm", [P, NT], F32)
    inv = small("inv", [P, NT], F32)
    mv1 = small("mv1", [P, NT, 2], F32)
    sd1 = small("sd1", [P, NT], F32)
    rs1 = small("rs1", [P, NT], F32)
    shift = small("shift", [P, NT], F32)
    hot_gen = place("hot_gen", [P, NT * 50], BF16, "hot")
    src_gen = place("src_gen", [P, P], BF16, "hot", 1024)
    deg_sum = small("deg_sum", [P, NT], F32)
    blk0 = small("blk0", [P, 25], F32)
    xn = place("xn", [TQ, 2, D], F32, "xn")

    with ExitStack() as ctx:
        bank = [ctx.enter_context(nc.psum_tensor(f"bank{i}", [P, 512], F32)) for i in range(8)]

        def bf(i):
            return bank[i][:, :].bitcast(BF16)

        def sem(name):
            return ctx.enter_context(nc.semaphore(name))

        const_done = sem("const_done")
        edges_in = sem("edges_in")
        LN_GROUPS = [(0, 1), (1, 2), (2, 4), (4, NT)]
        x_in = [sem(f"x_in{a}") for a, _ in LN_GROUPS]
        w_neigh_in = sem("w_neigh_in")
        w_self_in = sem("w_self_in")
        bias_in = sem("bias_in")
        raw_in = [sem(f"raw_in{i}") for i in range(RAWS)]
        out_done = sem("out_done")
        prep = sem("prep")
        edges_T = sem("edges_T")
        bn_done = sem("bn_done")
        stats = sem("stats")
        root = sem("root")
        rstd = sem("rstd")
        normed = sem("normed")
        xn_T = sem("xn_T")
        xnT_done = sem("xnT_done")
        y_ready = sem("y_ready")
        z_ready = sem("z_ready")
        yhi_done = sem("yhi_done")
        ylo_done = sem("ylo_done")
        z_out = sem("z_out")
        z_done = sem("z_done")
        src_wide = sem("src_wide")
        hot_made = sem("hot_made")
        hot_used = sem("hot_used")
        block_done = sem("block_done")
        block_out = sem("block_out")
        abs_done = sem("abs_done")
        scales = sem("scales")
        above = sem("above")
        ternary = sem("ternary")

        SLOTS = 8 * NT
        FIRST = 6

        def chunks_in(slot):
            def upto(s):
                return 0 if s < FIRST else min(NC, -(-NC * (s - FIRST + 1) // (SLOTS - FIRST)))
            return range(upto(slot - 1), upto(slot))

        def window(c):
            k, off = divmod(STEP * c - LEAD, WIN)
            parts = [(k, off, 0, WIN - off), (k + 1, 0, WIN - off, off)]
            return [p for p in parts if 0 <= p[0] < NB and p[3]]

        first_chunk = [min(c for c in range(NC) if any(p[0] == k for p in window(c))) for k in range(NB)]
        last_chunk = [max(c for c in range(NC) if any(p[0] == k for p in window(c))) for k in range(NB)]

        def blocks_ending(slot):
            return [k for k in range(NB) if last_chunk[k] in chunks_in(slot)]

        loads = []
        for w in (w_gate, w_up):
            for f in range(NF):
                loads.append((w[f * P:(f + 1) * P, :], KD))
        down_loads = [(2, 4), (2, 8), (3, 0), (3, 4), (3, 8), (2, 0)] + [(o, f) for o in (0, 1) for f in (0, 4, 8)]
        down_order = []
        for o, f in down_loads:
            n = min(4, NF - f)
            loads.append((w_down[o * P:(o + 1) * P, f * P:(f + n) * P], n))
            down_order += [(o, f + i) for i in range(n)]
        assert (2 * NF + 4) * P * 2 >= SBS * SB * P * 2
        job_load = [(l, i) for l, (_, n) in enumerate(loads) for i in range(n)]
        JOBS = len(job_load)
        load_end = [sum(n for _, n in loads[:l + 1]) for l in range(len(loads))]
        assert JOBS == 3 * NF * KD

        def tq_of(j):
            if j < 2 * NF * KD:
                return tq_gu[:, j // KD, (j % KD) * P:(j % KD + 1) * P]
            o, f = down_order[j - 2 * NF * KD]
            return tq_d[:, o, f * P:(f + 1) * P]

        def raw_of(j):
            l, i = job_load[j]
            return raw[:, l % RAWS, i * P:(i + 1) * P]

        LOADS1 = 2 * NF + 5
        JOBS1 = load_end[LOADS1 - 1]

        def jobs_in(slot, lag):
            def upto(s):
                return max(0, min(JOBS1, -(-JOBS1 * (s - lag + 1) // (SLOTS - 10))))
            return range(upto(slot - 1), upto(slot))

        GB, GC = 50, 32
        GK, GQ = N // GB, NCP // GC
        gen_hot = sem("gen_hot")
        gen_used = sem("gen_used")
        gen_out = sem("gen_out")
        gen_sum = sem("gen_sum")
        gen_taken = sem("gen_taken")

        deg_rows = sem("deg_rows")
        deg_row_out = sem("deg_row_out")
        deg_ready = sem("deg_ready")
        rdeg_done = sem("rdeg_done")
        n_ready = sem("n_ready")
        hsum = sem("hsum")
        leaky = sem("leaky")
        squares = sem("squares")
        norms = sem("norms")
        inv_done = sem("inv_done")
        x1_done = sem("x1_done")
        stats1 = sem("stats1")
        root1 = sem("root1")
        rstd1 = sem("rstd1")
        normed1 = sem("normed1")
        x1n_T = sem("x1n_T")
        def x1_bank(t):
            return bank[4 + t % 2 if t < 7 else 7]

        xhi_done = sem("xhi_done")
        xlo_done = sem("xlo_done")
        NL = len(loads) - LOADS1

        def down_jobs(a, b):
            lo, hi = (LOADS1 + max(0, min(NL, i)) for i in (a, b))
            return range(load_end[lo - 1], load_end[hi - 1])

        UNITS = [(0, 0), (0, 1), (1, 0), (1, 1), (0, 2), (1, 2)]
        UNITS += [(f, c) for f in range(2, NF - 1) for c in range(3)] + [(NF - 1, c) for c in (2, 0, 1)]
        NU = len(UNITS)
        assert NU == 3 * NF and CT[2][1] * TQ <= CW + CT[2][0] * TQ
        unit = {fc: u for u, fc in enumerate(UNITS)}
        first_of = [min(unit[f, c] for c in range(3)) for f in range(NF)]
        last_of = [max(unit[f, c] for c in range(3)) for f in range(NF)]
        LAG = 3
        TURN = ["G0", "U0", "D1", "G1", "U1", "D2", "G2", "U2", "D3", "G3", "U3", "D0"]

        def by_act(u, what):
            if what == "O":
                return u in (6, 8, 1, 4)
            return what in ("G0", "U0") or what in ("D1", "D2", "D3")[:max(0, min(3, NU - 1 - u))]

        def width(u):
            a, b = CT[UNITS[u][1]]
            return (b - a) * TQ

        def before(u):
            f, c = UNITS[u]
            return unit.get((f - 1, c))

        turn_of = {}
        pieces = []
        for n in range(NU + LAG):
            for what in TURN:
                u = n - LAG if what[0] == "D" else n
                if 0 <= u < NU:
                    pieces.append((u, what))
                    turn_of[u, what] = n
            for u in [NU - 3, NU - 2, NU - 1] if n == NU + LAG - 1 else []:
                for t in range(*CT[UNITS[u][1]]):
                    pieces.append((t, "O"))
                    turn_of[t, "O"] = n
        index = {p: i for i, p in enumerate(pieces)}
        RING = [2, 6, 0, 1, 5, 3, 4]
        added = {}
        for p in pieces:
            if by_act(*p) and (p[1] == "O" or p[1][0] == "D" and UNITS[p[0]][0]):
                added[p] = len(added) + 1
        out_of = {t: v for v in range(NU - 3, NU) for t in range(*CT[UNITS[v][1]])}
        stage = {}
        slot_before = {}
        for p in added:
            o = int(p[1][1]) - 1 if p[1] != "O" else len([q for q in stage if q[1] == "O"]) % 3
            same = [q for q in stage if stage[q][0] == o]
            stage[p] = (o, len(same) % 2)
            if len(same) >= 2:
                slot_before[p] = same[-2]
        took = {}
        for i, p in enumerate(pieces):
            took[p] = 1 + sum(by_act(*q) == by_act(*p) for q in pieces[:i])
        BANK7 = {(0, "U3"): ("X", 7), (1, "U1"): ("T", 1, 0), (1, "U3"): ("X", 8), (2, "U1"): ("T", 0, 1), (2, "U3"): ("X", 9),
                 (3, "U3"): ("T", 1, 1), (4, "U3"): ("T", 2, 0), (6, "U3"): ("T", 3, 0), (7, "U3"): ("T", 2, 1),
                 (8, "U3"): ("T", 3, 1)}
        for f in range(3, NF - 1):
            BANK7[first_of[f], "U3"] = ("T", f + 1, 0)
            BANK7[last_of[f], "U3"] = ("T", f + 1, 1)
        through7 = [("T", 0, 0)] + [BANK7[e] for e in sorted(BANK7)]
        turn_T = {e: i for i, e in enumerate(e for e in through7 if e[0] == "T")}
        piece_ready = sem("piece_ready")
        act_took = sem("act_took")
        dve_took = sem("dve_took")
        silu_done = sem("silu_done")
        h_done = sem("h_done")
        hhi_done = sem("hhi_done")
        hlo_done = sem("hlo_done")
        d_added = sem("d_added")
        t_ready = sem("t_ready")
        t_done = sem("t_done")

        def took_sem(u, what):
            return act_took if by_act(u, what) else dve_took

        def bank_of(u, what):
            return bank[RING[index[u, what] % len(RING)]]

        def nodes_of(u):
            a, b = CT[UNITS[u][1]]
            return slice(a * TQ, b * TQ)

        def job_of(u, what):
            f, k = UNITS[u][0], int(what[1])
            return {"G": KD * f + k, "U": KD * (NF + f) + k, "D": 2 * KD * NF + down_order.index((k, f))}[what[0]]

        def general_dve(dve):
            any_outside = dve.value_load(flag[0:1, 0:1])
            with dve.If(any_outside):
                dve.wait_ge(block_out, NB)
                dve.wait_ge(hot_used, NC - 1)
                dve.sem_inc(gen_out, 1)
                dve.sem_inc(gen_taken, 1)
                for sweep in range(2):
                    with dve.Fori(0, GQ) as q:
                        with dve.Fori(0, GK) as k:
                            cs = bass.ds(q * GC, GC)
                            dve.drain()
                            dve.wait_ge(gen_sum, 1 + (sweep * GQ + q) * NT)
                            nc.vector.tensor_scalar(tmp[:, 0:GC], dst_f[:, cs], blk0[:, bass.ds(k, 1)], None, ALU.subtract)
                            dve.drain()
                            nc.vector.tensor_scalar(win0[:, 0:GC], tmp[:, 0:GC], 0.0, None, ALU.is_ge)
                            dve.drain()
                            nc.vector.scalar_tensor_tensor(out=win0[:, 0:GC], in0=tmp[:, 0:GC], scalar=float(GB - 1),
                                                           in1=win0[:, 0:GC], op0=ALU.is_le, op1=ALU.mult)
                            nc.vector.scalar_tensor_tensor(out=key[:, 0:GC], in0=src_hi[:, cs], scalar=float(GB),
                                                           in1=tmp[:, 0:GC], op0=ALU.mult, op1=ALU.add)
                            dve.drain()
                            nc.vector.scalar_tensor_tensor(out=tmp[:, 0:GC], in0=key[:, 0:GC], scalar=1.0, in1=win0[:, 0:GC],
                                                           op0=ALU.add, op1=ALU.mult)
                            dve.drain()
                            nc.vector.tensor_scalar(key[:, 0:GC], tmp[:, 0:GC], 1.0, None, ALU.subtract)
                            dve.drain()
                            nc.vector.tensor_copy(tmp[:, 0:GC], src_lo[:, cs])
                            dve.drain()
                            done = ((sweep * GQ + q) * GK + k) * GC
                            for j in range(GC):
                                dve.wait_ge(gen_used, 1 + done + j)
                                nc.vector.tensor_scalar(src_gen[:, 0:TP], iota[:, 0:TP], tmp[:, j:j + 1], None, ALU.is_equal)
                                nc.vector.tensor_scalar(hot_gen[:, 0:NT * GB], iota[:, 0:NT * GB], key[:, j:j + 1], None,
                                                        ALU.is_equal).then_inc(gen_hot, 1)
                            dve.wait_ge(gen_used, 1 + done + GC)
                            for s in range(NT):
                                last = nc.vector.tensor_scalar(a_t[:, s, bass.ds(k * GB, GB)], bank[7][0:TP, s * GB:(s + 1) * GB],
                                                               1.0, None, ALU.mult)
                            last.then_inc(gen_out, 1)
                        for t in range(NT):
                            dve.wait_ge(gen_sum, 1 + (sweep * GQ + q) * NT + t + 1)
                            if sweep == 0:
                                nc.vector.tensor_copy(tmp[0:TP, 0:1], bank[6][0:TP, 0:1])
                                dve.drain()
                                nc.vector.tensor_tensor(deg_sum[0:TP, t:t + 1], deg_sum[0:TP, t:t + 1], tmp[0:TP, 0:1],
                                                        ALU.add).then_inc(gen_taken, 1)
                            else:
                                nc.vector.scalar_tensor_tensor(out=z[:, t, :], in0=bank[6][0:TP, :], scalar=deg_sum[0:TP, t:t + 1],
                                                               in1=z[:, t, :], op0=ALU.mult, op1=ALU.add).then_inc(gen_taken, 1)
                    if sweep == 0:
                        dve.drain()
                        nc.vector.tensor_scalar(rdeg[0:TP, :], deg_sum[0:TP, :], 1.0, None, ALU.max)
                        dve.drain()
                        nc.vector.reciprocal(deg_sum[0:TP, :], rdeg[0:TP, :])
                        dve.drain()

        def general_pe(pe):
            any_outside = pe.value_load(flag[0:1, 0:1])
            with pe.If(any_outside):
                pe.wait_ge(z_done, NT)
                pe.wait_ge(ylo_done, NT)
                pe.sem_inc(gen_used, 1)
                pe.sem_inc(gen_sum, 1)
                for sweep in range(2):
                    with pe.Fori(0, GQ) as q:
                        with pe.Fori(0, GK) as k:
                            done = ((sweep * GQ + q) * GK + k) * GC
                            pe.wait_ge(gen_out, 1 + (sweep * GQ + q) * GK + k)
                            for j in range(GC):
                                pe.wait_ge(gen_hot, done + j + 1)
                                nc.tensor.matmul(bank[7][0:TP, 0:NT * GB], src_gen[:, 0:TP], hot_gen[:, 0:NT * GB],
                                                 start=j == 0, stop=j == GC - 1).then_inc(gen_used, 1)
                        pe.wait_ge(gen_out, 1 + (sweep * GQ + q + 1) * GK)
                        for t in range(NT):
                            pe.wait_ge(gen_taken, 1 + (sweep * GQ + q) * NT + t)
                            if sweep == 0:
                                for s in range(NT):
                                    last = nc.tensor.matmul(bank[6][0:TP, 0:2], a_t[:, s, t * TP:(t + 1) * TP], ones_r[0:TP, :],
                                                            start=s == 0, stop=s == NT - 1)
                            else:
                                for s in range(NT):
                                    for y in (y_hi, y_lo):
                                        last = nc.tensor.matmul(bank[6][0:TP, :], a_t[:, s, t * TP:(t + 1) * TP], y[:, s, :],
                                                                start=s == 0 and y is y_hi, stop=s == NT - 1 and y is y_lo)
                            last.then_inc(gen_sum, 1)

        block = ctx.enter_context(nc.Block())

        @block.sync
        def _(sp):
            def load_x(g):
                a, b = LN_GROUPS[g]
                rows = x[a * TP:b * TP, :].rearrange("(t p) d -> p t d", p=TP)
                sp.dma_start(x_sb[0:112, a:b, :], rows[0:112]).then_inc(x_in[g], 16)
                sp.dma_start(x_sb[112:TP, a:b, :], rows[112:TP]).then_inc(x_in[g], 16)

            load_x(0)
            sp.dma_start(w_sb[:, :, 0:D], w_neigh.rearrange("(k p) n -> p k n", p=P)).then_inc(w_neigh_in, 16)
            sp.wait_ge(const_done, 1)
            for i, v in enumerate((src, dst)):
                sp.dma_start(e_i[:, 2 * i, :], v[0:P * P].rearrange("(c e) -> c e", e=P)).then_inc(edges_in, 16)
                n = E // P - P
                sp.dma_start(e_i[0:n, 2 * i + 1, :], v[P * P:(P + n) * P].rearrange("(c e) -> c e", e=P)).then_inc(edges_in, 16)
                sp.dma_start(e_i[n:n + 1, 2 * i + 1, 0:E - (P + n) * P],
                             v[(P + n) * P:E].rearrange("(c e) -> c e", c=1)).then_inc(edges_in, 16)
            load_x(1)
            sp.dma_start(w_sb[:, :, D:2 * D], w_self.rearrange("(k p) n -> p k n", p=P)).then_inc(w_self_in, 16)
            load_x(2)
            load_x(3)
            sp.dma_start(bias_b[:, :], bias.rearrange("(a n) -> a n", a=1).to_broadcast([P, D])).then_inc(bias_in, 16)
            for l, (w, n) in enumerate(loads):
                if l >= RAWS:
                    sp.wait_ge(ternary, load_end[l - RAWS])
                sp.dma_start(raw[:, l % RAWS, 0:n * P], w).then_inc(raw_in[l % RAWS], 16)
            for t, what in pieces:
                if what == "O":
                    if by_act(t, what):
                        sp.wait_ge(d_added, added[t, what])
                    else:
                        sp.wait_ge(dve_took, took[t, what])
                    sp.dma_start(out[t * TP:(t + 1) * TP, :], x_sb[:, t, :]).then_inc(out_done, 16)
            sp.wait_ge(out_done, 16 * NT)

        @block.gpsimd
        def _(pool):
            nc.gpsimd.memset(e_i[:], -1).then_inc(const_done, 1)
            nc.gpsimd.memset(ident[:], 1.0).then_inc(const_done, 1)
            nc.gpsimd.memset(ident_b[:], 1.0).then_inc(const_done, 1)
            pool.wait_ge(const_done, 3)
            for m in (ident, ident_b):
                nc.gpsimd.affine_select(out=m[:], in_=m[:], compare_op=ALU.is_equal, fill=0.0, base=0,
                                        pattern=[[-1, P]], channel_multiplier=1).then_inc(const_done, 1)
            nc.gpsimd.iota(win0[:], pattern=[[STEP, NCP]], base=-LEAD, channel_multiplier=0,
                           allow_small_or_imprecise_dtypes=True).then_inc(const_done, 1)
            nc.gpsimd.iota(iota[:], pattern=[[1, 512]], base=0, channel_multiplier=0,
                           allow_small_or_imprecise_dtypes=True).then_inc(const_done, 1)
            nc.gpsimd.iota(blk0[:], pattern=[[GB, GK]], base=0, channel_multiplier=0,
                           allow_small_or_imprecise_dtypes=True).then_inc(const_done, 1)
            nc.gpsimd.memset(ones[:], 1.0).then_inc(const_done, 1)
            nc.gpsimd.memset(eps[:], LN_EPS).then_inc(const_done, 1)
            nc.gpsimd.memset(deg_sum[:], 0.0).then_inc(const_done, 1)
            nc.gpsimd.memset(xn[:], 0.0).then_inc(const_done, 1)
            step = [0]

            def above_of(l):
                js = slice(load_end[l] - loads[l][1], load_end[l])
                pool.wait_ge(abs_done, load_end[l])
                nc.gpsimd.tensor_scalar(nscale[:, js], absum[:, js], -1.0 / P, -Q_EPS, ALU.mult, ALU.add).then_inc(scales, 1)
                pool.wait_ge(scales, step[0] + 1)
                nc.gpsimd.tensor_scalar(th_hi[:, js], nscale[:, js], -0.5, 0.0, ALU.mult, ALU.add).then_inc(scales, 1)
                nc.gpsimd.tensor_scalar(th_lo[:, js], nscale[:, js], 0.5, 0.0, ALU.mult, ALU.add).then_inc(scales, 1)
                step[0] += 3
                pool.wait_ge(scales, step[0])
                for j in range(js.start, js.stop):
                    nc.gpsimd.tensor_scalar(tq_of(j), raw_of(j), th_hi[:, j:j + 1], None, ALU.is_gt).then_inc(above, 1)

            for slot in range(SLOTS + 8):
                t, i = divmod(slot, 8)
                for j in jobs_in(slot, 7):
                    l, g = job_load[j]
                    if g == loads[l][1] - 1:
                        above_of(l)
                if i == 4 and 1 <= t <= NT:
                    if t == 1:
                        pool.wait_ge(bias_in, 16)
                    pool.wait_ge(z_out, t)
                    nc.gpsimd.tensor_tensor(z[:, t - 1, :], z[:, t - 1, :], bias_b[0:TP, :], ALU.add).then_inc(z_done, 1)
            for l in range(LOADS1, len(loads)):
                above_of(l)

            for n in range(NU + LAG):
                if 1 <= n <= NU:
                    u = n - 1
                    w = width(u)
                    pool.wait_ge(silu_done, u + 1)
                    pool.wait_ge(dve_took, took[u, "U3"])
                    if u >= 2:
                        pool.wait_ge(hlo_done, u - 1)
                    nc.gpsimd.tensor_tensor(hh[:, u % 2, 0:w], sg[:, u % 2, 0:w], u_acc[:, u % 2, 0:w], ALU.mult).then_inc(h_done, 1)
                for u, what in added:
                    if turn_of[u, what] != n:
                        continue
                    p = (u, what)
                    o, slot = stage[p]
                    pool.wait_ge(act_took, took[p])
                    if what == "O":
                        nc.gpsimd.tensor_tensor(x_sb[:, u, :], x_sb[:, u, :], d_one[0:TP, o, slot, 0:D], ALU.add).then_inc(d_added, 1)
                    else:
                        if (before(u), what) in added:
                            pool.wait_ge(d_added, added[before(u), what])
                        to = acc[:, o + 1, nodes_of(u)]
                        nc.gpsimd.tensor_tensor(to, to, d_one[:, o, slot, 0:width(u)], ALU.add).then_inc(d_added, 1)

        @block.scalar
        def _(act):
            def layernorm_root(g, ready, var, sdev, done):
                a, b = g
                act.wait_ge(ready, b)
                nc.scalar.activation(sdev[0:TP, a:b], var[0:TP, a:b, 1], ACT.Sqrt, bias=eps[0:TP, :]).then_inc(done, 1)

            def spread_src(b):
                if b >= SBS:
                    act.wait_ge(hot_used, SB * (b - SBS + 1))
                n = min(SB, NC - SB * b)
                nc.scalar.activation(hot_src[:, b % SBS, 0:n, 0:TP],
                                     src_lo[:, SB * b:SB * b + n, None].to_broadcast([P, n, TP]), ACT.Copy).then_inc(src_wide, 1)

            def batches_in(slot):
                cs = chunks_in(slot + 3)
                return [c // SB for c in cs if c % SB == 0]

            def abs_of(j):
                l, _ = job_load[j]
                act.wait_ge(raw_in[l % RAWS], 16 * (l // RAWS + 1))
                nc.scalar.activation(tq_of(j), raw_of(j), ACT.Abs, accum_out=absum[:, j:j + 1]).then_inc(abs_done, 1)

            act.wait_ge(const_done, 12)
            for slot in range(SLOTS + 8):
                t, i = divmod(slot, 8)
                if slot == FIRST - 3:
                    act.wait_ge(prep, 6)
                for b in batches_in(slot):
                    spread_src(b)
                if slot == 0:
                    nc.scalar.activation(nrm[:, 0:1], eps[:], ACT.Sqrt)
                    layernorm_root(LN_GROUPS[0], stats, mv, sd, root)
                    act.wait_ge(xn_T, 1)
                    nc.scalar.activation(xnT[:, 0, 0:KD * TP], bank[3][:, 0:KD * TP], ACT.Copy).then_inc(xnT_done, 1)
                    layernorm_root(LN_GROUPS[1], stats, mv, sd, root)
                if slot == 6:
                    layernorm_root(LN_GROUPS[2], stats, mv, sd, root)
                if slot == 11:
                    layernorm_root(LN_GROUPS[3], stats, mv, sd, root)
                if i == 1 and 1 <= t <= NT:
                    act.wait_ge(y_ready, t)
                    nc.scalar.activation(y_hi[:, t - 1, :], bank[4 + (t - 1) % 2][0:TP, :], ACT.Copy).then_inc(yhi_done, 1)
                if i == 2 and 1 <= t <= NT:
                    act.wait_ge(z_ready, t)
                    nc.scalar.activation(z[:, t - 1, :], bank[6 + (t - 1) % 2][0:TP, :], ACT.Copy).then_inc(z_out, 1)
                if i == 5 and t + 1 < NT:
                    act.wait_ge(xn_T, t + 2)
                    nc.scalar.activation(xnT[:, t + 1, 0:KD * TP], bank[3][:, 0:KD * TP], ACT.Copy).then_inc(xnT_done, 1)
                if slot < SLOTS:
                    for j in jobs_in(slot, 6):
                        abs_of(j)
                    for k in blocks_ending(slot):
                        act.wait_ge(block_done, k + 1)
                        n = min(WIN, N - k * WIN)
                        nc.scalar.activation(
                            a_t[:, :, k * WIN:k * WIN + n],
                            bank[k % 3][0:TP, 0:NT * WIN].rearrange("p (s d) -> p s d", d=WIN)[:, :, 0:n],
                            ACT.Copy).then_inc(block_out, 1)
            for c, (s0, n) in enumerate(ROW):
                act.wait_ge(deg_rows, c + 1)
                nc.scalar.activation(deg_row[:, s0:s0 + n], bank[ROW_BANK[c]][0:2, 0:n], ACT.Copy).then_inc(deg_row_out, 1)

            def root_of(t):
                act.wait_ge(stats1, t + 1)
                nc.scalar.activation(sd1[0:TP, t:t + 1], mv1[0:TP, t:t + 1, 1], ACT.Sqrt, bias=eps[0:TP, :]).then_inc(root1, 1)

            def normalize1(t):
                act.wait_ge(rstd1, 2 * t + 2)
                if t >= 2:
                    act.wait_ge(x1n_T, t - 1)
                nc.scalar.activation(xn[0:TP, t % 2, :], x_sb[:, t, :], ACT.Identity, bias=shift[0:TP, t:t + 1],
                                     scale=rs1[0:TP, t:t + 1]).then_inc(normed1, 1)

            def x1_high(t):
                act.wait_ge(x1n_T, t + 1)
                nc.scalar.activation(x1_hi[:, t, :, :].rearrange("p k s -> p (k s)"), x1_bank(t)[:, 0:KD * TQ],
                                     ACT.Copy).then_inc(xhi_done, 1)

            def ternary_out(f, down):
                act.wait_ge(t_ready, turn_T["T", f, down] + 1)
                if f >= 2:
                    act.wait_ge(piece_ready, index[last_of[f - 2], "D0" if down else "U3"] + 1)
                if not down:
                    nc.scalar.activation(t_gu[:, f % 2, :, :].rearrange("p a d -> p (a d)"), bf(7)[:, 0:2 * D],
                                         ACT.Copy).then_inc(t_done, 1)
                else:
                    nc.scalar.activation(t_d[:, f % 2, :], bf(7)[:, 0:D], ACT.Copy).then_inc(t_done, 1)

            for n in range(NT):
                for j in down_jobs(0 if n == 0 else n + 1, n + 2):
                    abs_of(j)
                if n == NT - 1:
                    act.wait_ge(n_ready, NT)
                    ternary_out(0, 0)
                act.wait_ge(leaky, n + 1)
                if n >= 1:
                    act.wait_ge(squares, n)
                nc.scalar.activation(bank[3][0:TP, :], z[:, n, :], ACT.Square, accum_out=ss[0:TP, n:n + 1]).then_inc(squares, 1)
                act.wait_ge(squares, n + 1)
                nc.scalar.activation(nrm[0:TP, n:n + 1], ss[0:TP, n:n + 1], ACT.Sqrt).then_inc(norms, 1)
                if n >= 1:
                    root_of(n - 1)
                if n == NT - 1:
                    normalize1(n - 2)
                    x1_high(n - 3)
                else:
                    if n >= 3:
                        x1_high(n - 3)
                    if n >= 2:
                        normalize1(n - 2)

            def take(u, what, to):
                act.wait_ge(piece_ready, index[u, what] + 1)
                j = job_of(u, what)
                nc.scalar.activation(to, bank_of(u, what)[:, 0:width(u)], ACT.Copy, scale=nscale[:, j:j + 1]).then_inc(act_took, 1)

            for n in range(NU + LAG):
                if n < NU:
                    w = width(n)
                    if n >= 2:
                        act.wait_ge(silu_done, n - 1)
                    take(n, "G0", g_acc[:, n % 2, 0:w])
                    if n >= 2:
                        act.wait_ge(h_done, n - 1)
                    take(n, "U0", u_acc[:, n % 2, 0:w])
                if n == 0:
                    normalize1(NT - 2)
                    x1_high(7)
                if n == 1:
                    root_of(NT - 1)
                if n == 2:
                    normalize1(NT - 1)
                if 1 <= n <= NU:
                    u = n - 1
                    wu = width(u)
                    act.wait_ge(dve_took, took[u, "G3"])
                    nc.scalar.activation(sg[:, u % 2, 0:wu], g_acc[:, u % 2, 0:wu], ACT.Silu).then_inc(silu_done, 1)
                for what in ("D1", "D2", "D3"):
                    v = n - LAG
                    if 0 <= v and by_act(v, what):
                        o = int(what[1])
                        if (v, what) not in added:
                            take(v, what, acc[:, o, nodes_of(v)])
                        else:
                            if (v, what) in slot_before:
                                act.wait_ge(d_added, added[slot_before[v, what]])
                            take(v, what, d_one[:, o - 1, stage[v, what][1], 0:width(v)])
                    if what == "D2" and n - 1 > 4 and (n - 1, "U3") in BANK7:
                        ternary_out(*BANK7[n - 1, "U3"][1:])
                    if what == "D2" and 1 <= n <= NU:
                        act.wait_ge(h_done, u + 1)
                        if u >= h_slots:
                            act.wait_ge(piece_ready, index[u - h_slots, "D0"] + 1)
                        nc.scalar.activation(h_hi[:, u % h_slots, 0:wu], hh[:, u % 2, 0:wu], ACT.Copy).then_inc(hhi_done, 1)
                if n == 1:
                    ternary_out(1, 0)
                    x1_high(8)
                elif n == 2:
                    ternary_out(0, 1)
                    x1_high(9)
                elif n in (3, 4) and (n, "U3") in BANK7:
                    ternary_out(*BANK7[n, "U3"][1:])
                for p in added:
                    if p[1] == "O" and turn_of[p] == n:
                        o, slot = stage[p]
                        if p in slot_before:
                            act.wait_ge(d_added, added[slot_before[p]])
                        act.wait_ge(piece_ready, index[p] + 1)
                        nc.scalar.activation(d_one[0:TP, o, slot, 0:D], bank_of(*p)[0:TP, :], ACT.Copy).then_inc(act_took, 1)

        @block.vector
        def _(dve):
            steps = [0]

            def link(ins):
                steps[0] += 1
                ins.then_inc(prep, 1)
                dve.wait_ge(prep, steps[0])

            def normalize(t):
                if t >= 2:
                    dve.wait_ge(xn_T, t - 1)
                nc.vector.tensor_scalar(xn[0:TP, t % 2, :], x_sb[:, t, :], mv[0:TP, t, 0:1], rs[0:TP, t:t + 1],
                                        ALU.subtract, ALU.mult).then_inc(normed, 1)

            def statistics(g):
                dve.wait_ge(x_in[LN_GROUPS.index(g)], 32)
                for t in range(*g):
                    nc.vector.bn_stats(bn[0:TP, t, :], x_sb[:, t, :]).then_inc(bn_done, 1)
                for t in range(*g):
                    dve.wait_ge(bn_done, t + 1)
                    nc.vector.bn_aggr(mv[0:TP, t, :], bn[0:TP, t, :]).then_inc(stats, 1)

            def reciprocals(i):
                a, b = LN_GROUPS[i]
                dve.wait_ge(root, i + 1)
                nc.vector.reciprocal(rs[0:TP, a:b], sd[0:TP, a:b]).then_inc(rstd, 1)
                dve.wait_ge(rstd, i + 1)

            def ternary_of(j):
                dve.wait_ge(above, j + 1)
                nc.vector.scalar_tensor_tensor(out=tq_of(j), in0=raw_of(j), scalar=th_lo[:, j:j + 1], in1=tq_of(j),
                                               op0=ALU.is_lt, op1=ALU.subtract).then_inc(ternary, 1)

            dve.wait_ge(const_done, 12)
            nc.vector.tensor_copy(ones_r[:], ones[:, 0:2]).then_inc(prep, 1)
            steps[0] += 1
            statistics(LN_GROUPS[0])
            reciprocals(0)
            normalize(0)
            dve.wait_ge(edges_in, 96)
            nc.vector.tensor_copy(e_f[:], e_i[:]).then_inc(prep, 1)
            steps[0] += 1
            statistics(LN_GROUPS[1])
            dve.wait_ge(edges_T, 1)
            srcs, dsts = bank[5][:, 0:NCP], bank[5][:, NCP:2 * NCP]
            nc.vector.tensor_copy(dst_f[:], dsts).then_inc(prep, 1)
            steps[0] += 1
            link(nc.vector.tensor_scalar(tmp[:], srcs, (TP - 1) / 2, 1.0 / TP, ALU.subtract, ALU.mult))
            link(nc.vector.tensor_scalar(src_hi[:], tmp[:], ROUND, ROUND, ALU.add, ALU.subtract))
            link(nc.vector.scalar_tensor_tensor(out=src_lo[:], in0=src_hi[:], scalar=-float(TP), in1=srcs, op0=ALU.mult, op1=ALU.add))
            link(nc.vector.tensor_tensor(tmp[:], dst_f[:], win0[:], ALU.subtract))
            link(nc.vector.tensor_scalar(key[:], tmp[:], 0.0, None, ALU.is_ge))
            link(nc.vector.scalar_tensor_tensor(out=win0[:], in0=tmp[:], scalar=float(WIN - 1), in1=key[:], op0=ALU.is_le,
                                                op1=ALU.mult, accum_out=inside[:]))
            link(nc.vector.scalar_tensor_tensor(out=key[:], in0=src_hi[:], scalar=float(WIN), in1=tmp[:], op0=ALU.mult, op1=ALU.add))
            link(nc.vector.scalar_tensor_tensor(out=tmp[:], in0=key[:], scalar=1.0, in1=win0[:], op0=ALU.add, op1=ALU.mult))
            link(nc.vector.tensor_scalar(key[:], tmp[:], 1.0, None, ALU.subtract))
            reciprocals(1)
            normalize(1)
            dve.wait_ge(edges_T, 2)
            nc.vector.tensor_scalar(good[:], bank[5][:, 2 * NCP:2 * NCP + 1], float(E), None, ALU.is_equal).then_inc(prep, 1)
            nc.vector.tensor_scalar(flag[:], bank[5][:, 2 * NCP:2 * NCP + 1], float(E), None, ALU.is_lt).then_inc(prep, 1)
            steps[0] += 2

            for slot in range(SLOTS + 8):
                t, i = divmod(slot, 8)
                if slot == 5:
                    statistics(LN_GROUPS[2])
                if slot == 7:
                    reciprocals(2)
                if slot == 10:
                    statistics(LN_GROUPS[3])
                if slot == 12:
                    reciprocals(3)
                if i == 0 and 1 <= t and t + 1 < NT:
                    normalize(t + 1)
                if i == 2 and 1 <= t <= NT:
                    dve.wait_ge(yhi_done, t)
                    nc.vector.tensor_tensor(y_lo[:, t - 1, :], bank[4 + (t - 1) % 2][0:TP, :],
                                            y_hi[:, t - 1, :].bitcast(F32), ALU.subtract).then_inc(ylo_done, 1)
                if slot < SLOTS:
                    for c in chunks_in(slot + 1):
                        if c % SB == 0:
                            b, n = c // SB, min(SB, NC - c)
                            dve.wait_ge(src_wide, b + 1)
                            nc.vector.tensor_tensor(hot_src[:, b % SBS, 0:n, 0:TP], iota[:, None, 0:TP].to_broadcast([P, n, TP]),
                                                    hot_src[:, b % SBS, 0:n, 0:TP], ALU.is_equal)
                        if c >= HOT:
                            dve.wait_ge(hot_used, c - HOT + 1)
                        nc.vector.tensor_scalar(hot_dst[:, c % HOT, :], iota[:, 0:NT * WIN], key[:, c:c + 1], None,
                                                ALU.is_equal).then_inc(hot_made, 1)
                for j in jobs_in(slot, 10):
                    ternary_of(j)

            general_dve(dve)

            dve.wait_ge(deg_ready, 1)
            nc.vector.tensor_scalar(rdeg[0:TP, :], bank[2][0:TP, 0:NT], 1.0, None, ALU.max).then_inc(rdeg_done, 1)
            dve.wait_ge(rdeg_done, 1)
            nc.vector.reciprocal(rs[0:TP, :], rdeg[0:TP, :]).then_inc(rdeg_done, 1)
            dve.wait_ge(rdeg_done, 2)
            nc.vector.tensor_scalar(rdeg[0:TP, :], rs[0:TP, :], good[0:TP, :], None, ALU.mult).then_inc(rdeg_done, 1)
            dve.wait_ge(rdeg_done, 3)

            def neighbour_sum(t):
                dve.wait_ge(n_ready, t + 1)
                dve.wait_ge(z_done, t + 1)
                nc.vector.scalar_tensor_tensor(out=z[:, t, :], in0=bank[t % 2][0:TP, :], scalar=rdeg[0:TP, t:t + 1],
                                               in1=z[:, t, :], op0=ALU.mult, op1=ALU.add).then_inc(hsum, 1)

            def leak(t):
                dve.wait_ge(hsum, t + 1)
                nc.vector.scalar_tensor_tensor(out=z[:, t, :], in0=z[:, t, :], scalar=SLOPE, in1=z[:, t, :],
                                               op0=ALU.mult, op1=ALU.max).then_inc(leaky, 1)

            def residual(t, between=None):
                dve.wait_ge(norms, t + 1)
                nc.vector.tensor_scalar(nrm[0:TP, t:t + 1], nrm[0:TP, t:t + 1], NORM_EPS, None, ALU.max).then_inc(inv_done, 1)
                dve.wait_ge(inv_done, 2 * t + 1)
                nc.vector.reciprocal(inv[0:TP, t:t + 1], nrm[0:TP, t:t + 1]).then_inc(inv_done, 1)
                if between is not None:
                    leak(between)
                dve.wait_ge(inv_done, 2 * t + 2)
                nc.vector.scalar_tensor_tensor(out=x_sb[:, t, :], in0=z[:, t, :], scalar=inv[0:TP, t:t + 1],
                                               in1=x_sb[:, t, :], op0=ALU.mult, op1=ALU.add).then_inc(x1_done, 1)
                dve.wait_ge(x1_done, t + 1)
                nc.vector.bn_stats(bn[0:TP, t, :], x_sb[:, t, :]).then_inc(bn_done, 1)
                dve.wait_ge(bn_done, NT + t + 1)
                nc.vector.bn_aggr(mv1[0:TP, t, :], bn[0:TP, t, :]).then_inc(stats1, 1)

            def shift1(t):
                dve.wait_ge(root1, t + 1)
                nc.vector.reciprocal(rs1[0:TP, t:t + 1], sd1[0:TP, t:t + 1]).then_inc(rstd1, 1)
                dve.wait_ge(rstd1, 2 * t + 1)
                nc.vector.scalar_tensor_tensor(out=shift[0:TP, t:t + 1], in0=mv1[0:TP, t, 0:1], scalar=-1.0, in1=rs1[0:TP, t:t + 1],
                                               op0=ALU.mult, op1=ALU.mult).then_inc(rstd1, 1)

            def x1_low(t):
                dve.wait_ge(xhi_done, t + 1)
                nc.vector.tensor_tensor(x1_lo[:, t, 0:KD * TQ], x1_bank(t)[:, 0:KD * TQ],
                                        x1_hi[:, t, :, :].rearrange("p k s -> p (k s)").bitcast(F32),
                                        ALU.subtract).then_inc(xlo_done, 1)

            for n in range(NT):
                neighbour_sum(n)
                if n >= 1:
                    residual(n - 1, between=n)
                else:
                    leak(n)
                if n >= 2:
                    shift1(n - 2)
                if n >= 4:
                    x1_low(n - 4)
                for j in down_jobs(n - 1, n):
                    ternary_of(j)
            shift1(NT - 2)
            x1_low(6)

            def take(u, what):
                w, k, j = width(u), int(what[1]), job_of(u, what)
                to = {"G": g_acc[:, u % 2, 0:w], "U": u_acc[:, u % 2, 0:w], "D": acc[:, k, nodes_of(u)]}[what[0]]
                dve.wait_ge(piece_ready, index[u, what] + 1)
                if what in ("G1", "U1"):
                    dve.wait_ge(act_took, took[u, what[0] + "0"])
                elif what[0] != "D":
                    dve.wait_ge(dve_took, took[u, what[0] + str(k - 1)])
                elif (before(u), what) in added:
                    dve.wait_ge(d_added, added[before(u), what])
                elif UNITS[u][0]:
                    dve.wait_ge(dve_took, took[before(u), what])
                if what[0] == "D" and UNITS[u][0] == 0:
                    nc.vector.tensor_scalar(to, bank_of(u, what)[:, 0:w], nscale[:, j:j + 1], None, ALU.mult).then_inc(dve_took, 1)
                else:
                    nc.vector.scalar_tensor_tensor(out=to, in0=bank_of(u, what)[:, 0:w], scalar=nscale[:, j:j + 1], in1=to,
                                                   op0=ALU.mult, op1=ALU.add).then_inc(dve_took, 1)

            def low_of_h(u):
                w = width(u)
                dve.wait_ge(hhi_done, u + 1)
                nc.vector.tensor_tensor(h_lo[:, u % h_slots, 0:w], hh[:, u % 2, 0:w], h_hi[:, u % h_slots, 0:w].bitcast(F32),
                                        ALU.subtract).then_inc(hlo_done, 1)

            for n in range(NU + LAG):
                for what in TURN:
                    u = n - LAG if what[0] == "D" else n
                    if 0 <= u < NU and not by_act(u, what):
                        take(u, what)
                    if n == 3 and what == "U1":
                        x1_low(9)
                if n == 0:
                    residual(NT - 1)
                    x1_low(7)
                if n == 1:
                    shift1(NT - 1)
                    x1_low(8)
                if 1 <= n <= NU:
                    low_of_h(n - 1)
                for t, what in pieces:
                    if what == "O" and n == turn_of[t, what] and not by_act(t, what):
                        dve.wait_ge(piece_ready, index[t, what] + 1)
                        nc.vector.tensor_tensor(x_sb[:, t, :], bank_of(t, what)[0:TP, :], x_sb[:, t, :],
                                                ALU.add).then_inc(dve_took, 1)

        @block.tensor
        def _(pe):
            def transpose_xn(t, ready, to, done, n=TP):
                pe.wait_ge(ready, t + 1)
                for k in range(KD):
                    last = nc.tensor.transpose(to[:, k * n:(k + 1) * n], xn[0:n, t % 2, k * P:(k + 1) * P], ident[0:n, 0:n])
                last.then_inc(done, 1)

            def add_chunk(c):
                pe.wait_ge(hot_made, c + 1)
                parts = window(c)
                for k, d0, w0, n in parts:
                    if c == first_chunk[k] and k >= 3:
                        pe.wait_ge(block_out, k - 2)
                    last = nc.tensor.matmul(
                        bank[k % 3][0:TP, 0:NT * WIN].rearrange("p (s d) -> p s d", d=WIN)[:, :, d0:d0 + n],
                        hot_src[:, c // SB % SBS, c % SB, 0:TP],
                        hot_dst[:, c % HOT, :].rearrange("p (s d) -> p s d", d=WIN)[:, :, w0:w0 + n],
                        start=c == first_chunk[k], stop=c == last_chunk[k], skip_group_check=True)
                    if c == last_chunk[k]:
                        last.then_inc(block_done, 1)
                    elif (k, d0, w0, n) == parts[-1]:
                        last.then_inc(hot_used, 1)

            pe.wait_ge(const_done, 12)
            transpose_xn(0, normed, bank[3], xn_T)
            for slot in range(SLOTS):
                t, i = divmod(slot, 8)
                if i == 0:
                    pe.wait_ge(xnT_done, t + 1)
                    if t == 0:
                        pe.wait_ge(w_neigh_in, 16)
                    if t == 1:
                        pe.wait_ge(prep, 14)
                    if t >= 2:
                        pe.wait_ge(ylo_done, t - 1)
                if i == 4 and t >= 2:
                    pe.wait_ge(z_out, t - 1)
                if slot == 4:
                    pe.wait_ge(w_self_in, 16)
                if slot == 1:
                    pe.wait_ge(prep, 2)
                    for e, (rows, col) in enumerate(((P, 0), (32, P), (P, NCP), (32, NCP + P))):
                        last = nc.tensor.transpose(bank[5][:, col:col + rows], e_f[0:rows, e, :], ident[0:rows, 0:rows])
                    last.then_inc(edges_T, 1)
                if slot == 5:
                    pe.wait_ge(prep, 9)
                    nc.tensor.matmul(bank[5][:, 2 * NCP:2 * NCP + 1], ones[:], inside[:], start=True, stop=True).then_inc(edges_T, 1)
                k, half = i % 4, i // 4
                to = bank[(6 if half else 4) + t % 2]
                last = nc.tensor.matmul(to[0:TP, :], xnT[:, t, k * TP:(k + 1) * TP], w_sb[:, k, half * D:(half + 1) * D],
                                        start=k == 0, stop=k == KD - 1)
                if k == KD - 1:
                    last.then_inc(z_ready if half else y_ready, 1)
                if i == 4 and t + 1 < NT:
                    transpose_xn(t + 1, normed, bank[3], xn_T)
                for c in chunks_in(slot):
                    add_chunk(c)

            def ternary_in(f, down):
                pe.wait_ge(ternary, JOBS if down else JOBS1)
                if not down:
                    for a in range(2):
                        for k in range(KD):
                            last = nc.tensor.transpose(bf(7)[:, a * D + k * P:a * D + (k + 1) * P],
                                                       tq_gu[:, a * NF + f, k * P:(k + 1) * P], ident_b[:])
                else:
                    for o in range(KD):
                        last = nc.tensor.transpose(bf(7)[:, o * P:(o + 1) * P], tq_d[:, o, f * P:(f + 1) * P], ident_b[:])
                last.then_inc(t_ready, 1)

            general_pe(pe)

            pe.wait_ge(prep, 1)
            for c, (s0, n) in enumerate(ROW):
                pe.wait_ge(block_out, NB if c == len(ROW) - 1 else max(-(-(s0 + n) // WIN), NB - 2))
                for s in range(NT):
                    last = nc.tensor.matmul(bank[ROW_BANK[c]][0:2, 0:n], ones_r[0:TP, :], a_t[:, s, s0:s0 + n],
                                            start=s == 0, stop=s == NT - 1)
                last.then_inc(deg_rows, 1)
            pe.wait_ge(ylo_done, NT)
            for n in range(NT):
                if n >= 2:
                    pe.wait_ge(hsum, n - 1)
                if n == 1:
                    pe.wait_ge(deg_row_out, len(ROW))
                    for t in range(NT):
                        last = nc.tensor.matmul(bank[2][0:TP, t:t + 1], deg_row[0:1, t * TP:(t + 1) * TP], ones[0:1, 0:1],
                                                start=True, stop=True, skip_group_check=True)
                    last.then_inc(deg_ready, 1)
                for s in range(NT):
                    for y in (y_hi, y_lo):
                        last = nc.tensor.matmul(bank[n % 2][0:TP, :], a_t[:, s, n * TP:(n + 1) * TP], y[:, s, :],
                                                start=s == 0 and y is y_hi, stop=s == NT - 1 and y is y_lo)
                last.then_inc(n_ready, 1)
                if 3 <= n:
                    t = n - 3
                    if t >= 2:
                        pe.wait_ge(xlo_done, t - 1)
                    transpose_xn(t, normed1, x1_bank(t), x1n_T, TQ)
                if n == NT - 2:
                    ternary_in(0, 0)

            def through_bank7(e):
                i = through7.index(e)
                if through7[i - 1][0] == "T":
                    pe.wait_ge(t_done, turn_T[through7[i - 1]] + 1)
                else:
                    pe.wait_ge(xlo_done, through7[i - 1][1] + 1)
                if e[0] == "T":
                    ternary_in(e[1], e[2])
                else:
                    transpose_xn(e[1], normed1, bank[7], x1n_T, TQ)

            for i, (u, what) in enumerate(pieces):
                if i >= len(RING):
                    old = pieces[i - len(RING)]
                    pe.wait_ge(took_sem(*old), took[old])
                else:
                    pe.wait_ge(*{2: (rdeg_done, 1), 6: (z_out, NT), 0: (hsum, NT - 1), 1: (hsum, NT), 5: (xlo_done, 6),
                                 3: (squares, NT), 4: (xlo_done, 7)}[RING[i]])
                if what == "O":
                    v = out_of[u]
                    pe.wait_ge(dve_took, took[v, "D0"])
                    for o in range(1, KD):
                        if by_act(v, f"D{o}"):
                            pe.wait_ge(d_added, added[v, f"D{o}"])
                    for k in range(KD):
                        last = nc.tensor.transpose(bank_of(u, what)[0:TP, k * P:(k + 1) * P], acc[:, k, u * TQ:u * TQ + TP], ident[:])
                    last.then_inc(piece_ready, 1)
                    continue
                f, c = UNITS[u]
                a, b = CT[c]
                k = int(what[1])
                if what == "G0":
                    if f == 0:
                        pe.wait_ge(xlo_done, b)
                    if u == first_of[f]:
                        pe.wait_ge(t_done, turn_T["T", f, 0] + 1)
                if what == "D1":
                    pe.wait_ge(hlo_done, u + 1)
                    if u == first_of[f]:
                        pe.wait_ge(t_done, turn_T["T", f, 1] + 1)
                if what[0] == "D":
                    w = t_d[:, f % 2, k * P:(k + 1) * P]
                    to = bank_of(u, what)[:, 0:width(u)]
                    parts = (h_hi[:, u % h_slots, 0:width(u)], h_lo[:, u % h_slots, 0:width(u)])
                else:
                    w = t_gu[:, f % 2, int(what[0] == "U"), k * P:(k + 1) * P]
                    to = bank_of(u, what)[:, 0:width(u)].rearrange("p (t s) -> p t s", s=TQ)
                    parts = (x1_hi[:, a:b, k, :], x1_lo[:, a:b, k * TQ:(k + 1) * TQ])
                for h in range(2):
                    last = nc.tensor.matmul(to, w, parts[h], start=h == 0, stop=h == 1)
                last.then_inc(piece_ready, 1)
                if (u, what) in BANK7:
                    through_bank7(BANK7[u, what])


_INS = ["x", "src", "dst", "L0_gnn_W_self", "L0_gnn_W_neigh", "L0_gnn_b", "L0_ffn_w_gate", "L0_ffn_w_up", "L0_ffn_w_down"]


def kernel(**inputs):
    import numpy as np
    import concourse.bacc as bacc
    from concourse.bass_utils import run_bass_kernel_spmd

    nc = bacc.Bacc("TRN2", target_bir_lowering=False, num_devices=1)
    arrays, args = {}, []
    for name in _INS:
        a = np.ascontiguousarray(inputs[name])
        arrays[f"in_{name}"] = a
        args.append(nc.dram_tensor(f"in_{name}", a.shape, mybir.dt.from_np(a.dtype), kind="ExternalInput").ap())
    shape = arrays["in_x"].shape
    args.append(nc.dram_tensor("out_x", shape, F32, kind="ExternalOutput").ap())
    gnn_ffn(nc, *args)
    r = run_bass_kernel_spmd(nc, [arrays], core_ids=[0])
    return r.results[0]["out_x"]
```
